# Optimizing a Trainium2 kernel written in Bass

```python
import numpy as np
import jax
import jax.numpy as jnp

def _softmax(x, axis=-1):
    return jax.nn.softmax(x, axis=axis)

def _gelu(x):
    return jax.nn.gelu(x, approximate=True)

def _silu(x):
    return jax.nn.silu(x)

def _sigmoid(x):
    return jax.nn.sigmoid(x)

def _layernorm(x, axis=-1, eps=1e-05):
    m = jnp.mean(x, axis=axis, keepdims=True)
    v = jnp.var(x, axis=axis, keepdims=True)
    return (x - m) / jnp.sqrt(v + eps)

def _scatter_add(tgt, idx, src, axis=0):
    return tgt.at[idx].add(src)

def _segment_sum(src, seg, n):
    return jax.ops.segment_sum(src, seg, n)
kernel_name = 'mk_dlrm_tower_d1_rec_r8_f53d0b'

def setup_inputs(seed: int=0):
    np.random.seed(seed)
    _w = jnp.asarray

    def _rec_inputs():
        import jax
        import jax.numpy as jnp
        _tk = jax.random.key(seed)
        dense_ctx = jax.random.normal(jax.random.fold_in(_tk, 190), (2048, 16), jnp.float32)
        ids = jnp.stack([jax.random.randint(jax.random.fold_in(_tk, 200 + f), (2048,), 0, v, jnp.int32) for f, v in enumerate([12500, 1000, 12500, 12500, 1250, 1250, 12500, 1250, 12500, 1000, 12500, 125000, 125000, 125000, 1000, 1250, 1250, 1250, 1250, 1000, 125000, 125000, 12500, 125000, 1000, 12500, 1000, 1250, 12500, 1000, 12500, 1000, 1000, 12500, 12500, 1000, 1250, 12500, 1250, 1000])], axis=1)
        tbl_0 = 0.05 * jax.random.normal(jax.random.fold_in(_tk, 500 + 0), (12500, 32), jnp.float32)
        tbl_1 = 0.05 * jax.random.normal(jax.random.fold_in(_tk, 500 + 1), (1000, 32), jnp.float32)
        tbl_2 = 0.05 * jax.random.normal(jax.random.fold_in(_tk, 500 + 2), (12500, 32), jnp.float32)
        tbl_3 = 0.05 * jax.random.normal(jax.random.fold_in(_tk, 500 + 3), (12500, 32), jnp.float32)
        tbl_4 = 0.05 * jax.random.normal(jax.random.fold_in(_tk, 500 + 4), (1250, 32), jnp.float32)
        tbl_5 = 0.05 * jax.random.normal(jax.random.fold_in(_tk, 500 + 5), (1250, 32), jnp.float32)
        tbl_6 = 0.05 * jax.random.normal(jax.random.fold_in(_tk, 500 + 6), (12500, 32), jnp.float32)
        tbl_7 = 0.05 * jax.random.normal(jax.random.fold_in(_tk, 500 + 7), (1250, 32), jnp.float32)
        tbl_8 = 0.05 * jax.random.normal(jax.random.fold_in(_tk, 500 + 8), (12500, 32), jnp.float32)
        tbl_9 = 0.05 * jax.random.normal(jax.random.fold_in(_tk, 500 + 9), (1000, 32), jnp.float32)
        tbl_10 = 0.05 * jax.random.normal(jax.random.fold_in(_tk, 500 + 10), (12500, 32), jnp.float32)
        tbl_11 = 0.05 * jax.random.normal(jax.random.fold_in(_tk, 500 + 11), (125000, 32), jnp.float32)
        tbl_12 = 0.05 * jax.random.normal(jax.random.fold_in(_tk, 500 + 12), (125000, 32), jnp.float32)
        tbl_13 = 0.05 * jax.random.normal(jax.random.fold_in(_tk, 500 + 13), (125000, 32), jnp.float32)
        tbl_14 = 0.05 * jax.random.normal(jax.random.fold_in(_tk, 500 + 14), (1000, 32), jnp.float32)
        tbl_15 = 0.05 * jax.random.normal(jax.random.fold_in(_tk, 500 + 15), (1250, 32), jnp.float32)
        tbl_16 = 0.05 * jax.random.normal(jax.random.fold_in(_tk, 500 + 16), (1250, 32), jnp.float32)
        tbl_17 = 0.05 * jax.random.normal(jax.random.fold_in(_tk, 500 + 17), (1250, 32), jnp.float32)
        tbl_18 = 0.05 * jax.random.normal(jax.random.fold_in(_tk, 500 + 18), (1250, 32), jnp.float32)
        tbl_19 = 0.05 * jax.random.normal(jax.random.fold_in(_tk, 500 + 19), (1000, 32), jnp.float32)
        tbl_20 = 0.05 * jax.random.normal(jax.random.fold_in(_tk, 500 + 20), (125000, 32), jnp.float32)
        tbl_21 = 0.05 * jax.random.normal(jax.random.fold_in(_tk, 500 + 21), (125000, 32), jnp.float32)
        tbl_22 = 0.05 * jax.random.normal(jax.random.fold_in(_tk, 500 + 22), (12500, 32), jnp.float32)
        tbl_23 = 0.05 * jax.random.normal(jax.random.fold_in(_tk, 500 + 23), (125000, 32), jnp.float32)
        tbl_24 = 0.05 * jax.random.normal(jax.random.fold_in(_tk, 500 + 24), (1000, 32), jnp.float32)
        tbl_25 = 0.05 * jax.random.normal(jax.random.fold_in(_tk, 500 + 25), (12500, 32), jnp.float32)
        tbl_26 = 0.05 * jax.random.normal(jax.random.fold_in(_tk, 500 + 26), (1000, 32), jnp.float32)
        tbl_27 = 0.05 * jax.random.normal(jax.random.fold_in(_tk, 500 + 27), (1250, 32), jnp.float32)
        tbl_28 = 0.05 * jax.random.normal(jax.random.fold_in(_tk, 500 + 28), (12500, 32), jnp.float32)
        tbl_29 = 0.05 * jax.random.normal(jax.random.fold_in(_tk, 500 + 29), (1000, 32), jnp.float32)
        tbl_30 = 0.05 * jax.random.normal(jax.random.fold_in(_tk, 500 + 30), (12500, 32), jnp.float32)
        tbl_31 = 0.05 * jax.random.normal(jax.random.fold_in(_tk, 500 + 31), (1000, 32), jnp.float32)
        tbl_32 = 0.05 * jax.random.normal(jax.random.fold_in(_tk, 500 + 32), (1000, 32), jnp.float32)
        tbl_33 = 0.05 * jax.random.normal(jax.random.fold_in(_tk, 500 + 33), (12500, 32), jnp.float32)
        tbl_34 = 0.05 * jax.random.normal(jax.random.fold_in(_tk, 500 + 34), (12500, 32), jnp.float32)
        tbl_35 = 0.05 * jax.random.normal(jax.random.fold_in(_tk, 500 + 35), (1000, 32), jnp.float32)
        tbl_36 = 0.05 * jax.random.normal(jax.random.fold_in(_tk, 500 + 36), (1250, 32), jnp.float32)
        tbl_37 = 0.05 * jax.random.normal(jax.random.fold_in(_tk, 500 + 37), (12500, 32), jnp.float32)
        tbl_38 = 0.05 * jax.random.normal(jax.random.fold_in(_tk, 500 + 38), (1250, 32), jnp.float32)
        tbl_39 = 0.05 * jax.random.normal(jax.random.fold_in(_tk, 500 + 39), (1000, 32), jnp.float32)
        _rk = jax.random.fold_in(_tk, 7)
        W_top1 = 0.0354441 * jax.random.normal(jax.random.fold_in(_tk, 801), (796, 512), jnp.float32)
        W_top2 = 0.0441942 * jax.random.normal(jax.random.fold_in(_tk, 802), (512, 256), jnp.float32)
        W_top3 = 0.0625 * jax.random.normal(jax.random.fold_in(_tk, 803), (256, 1), jnp.float32)
        b_top1 = jnp.zeros((512,), jnp.float32)
        b_top2 = jnp.zeros((256,), jnp.float32)
        return (dense_ctx, ids, tbl_0, tbl_1, tbl_2, tbl_3, tbl_4, tbl_5, tbl_6, tbl_7, tbl_8, tbl_9, tbl_10, tbl_11, tbl_12, tbl_13, tbl_14, tbl_15, tbl_16, tbl_17, tbl_18, tbl_19, tbl_20, tbl_21, tbl_22, tbl_23, tbl_24, tbl_25, tbl_26, tbl_27, tbl_28, tbl_29, tbl_30, tbl_31, tbl_32, tbl_33, tbl_34, tbl_35, tbl_36, tbl_37, tbl_38, tbl_39, W_top1, b_top1, W_top2, b_top2, W_top3)
    dense_ctx, ids, tbl_0, tbl_1, tbl_2, tbl_3, tbl_4, tbl_5, tbl_6, tbl_7, tbl_8, tbl_9, tbl_10, tbl_11, tbl_12, tbl_13, tbl_14, tbl_15, tbl_16, tbl_17, tbl_18, tbl_19, tbl_20, tbl_21, tbl_22, tbl_23, tbl_24, tbl_25, tbl_26, tbl_27, tbl_28, tbl_29, tbl_30, tbl_31, tbl_32, tbl_33, tbl_34, tbl_35, tbl_36, tbl_37, tbl_38, tbl_39, W_top1, b_top1, W_top2, b_top2, W_top3 = _rec_inputs()

    def _L0_rec_setup():
        import jax, jax.numpy as jnp
        import numpy as np
        NUM_FIELDS = 40
        _I_IDX, _J_IDX = np.triu_indices(NUM_FIELDS, k=1)
        key = jax.random.key(seed)
        k1, k2 = jax.random.split(key)
        batch, num_fields, embed_dim = (1024, NUM_FIELDS, 32)
        num_interactions = num_fields * (num_fields - 1) // 2
        embeddings = jax.random.normal(k1, (batch, num_fields, embed_dim), dtype=jnp.float32)
        W = jax.random.normal(k2, (num_interactions, embed_dim, embed_dim), dtype=jnp.float32)
        return {'embeddings': embeddings, 'W': W}
    _L0_rec_all = _L0_rec_setup()
    _L0_rec_in = {k: v for k, v in _L0_rec_all.items() if k in ('W',)}
    del _L0_rec_all
    return {'dense_ctx': dense_ctx, 'ids': ids, 'tbl_0': tbl_0, 'tbl_1': tbl_1, 'tbl_2': tbl_2, 'tbl_3': tbl_3, 'tbl_4': tbl_4, 'tbl_5': tbl_5, 'tbl_6': tbl_6, 'tbl_7': tbl_7, 'tbl_8': tbl_8, 'tbl_9': tbl_9, 'tbl_10': tbl_10, 'tbl_11': tbl_11, 'tbl_12': tbl_12, 'tbl_13': tbl_13, 'tbl_14': tbl_14, 'tbl_15': tbl_15, 'tbl_16': tbl_16, 'tbl_17': tbl_17, 'tbl_18': tbl_18, 'tbl_19': tbl_19, 'tbl_20': tbl_20, 'tbl_21': tbl_21, 'tbl_22': tbl_22, 'tbl_23': tbl_23, 'tbl_24': tbl_24, 'tbl_25': tbl_25, 'tbl_26': tbl_26, 'tbl_27': tbl_27, 'tbl_28': tbl_28, 'tbl_29': tbl_29, 'tbl_30': tbl_30, 'tbl_31': tbl_31, 'tbl_32': tbl_32, 'tbl_33': tbl_33, 'tbl_34': tbl_34, 'tbl_35': tbl_35, 'tbl_36': tbl_36, 'tbl_37': tbl_37, 'tbl_38': tbl_38, 'tbl_39': tbl_39, 'W_top1': W_top1, 'b_top1': b_top1, 'W_top2': W_top2, 'b_top2': b_top2, 'W_top3': W_top3, 'L0_rec_W': _L0_rec_in['W']}

def reference(dense_ctx, ids, tbl_0, tbl_1, tbl_2, tbl_3, tbl_4, tbl_5, tbl_6, tbl_7, tbl_8, tbl_9, tbl_10, tbl_11, tbl_12, tbl_13, tbl_14, tbl_15, tbl_16, tbl_17, tbl_18, tbl_19, tbl_20, tbl_21, tbl_22, tbl_23, tbl_24, tbl_25, tbl_26, tbl_27, tbl_28, tbl_29, tbl_30, tbl_31, tbl_32, tbl_33, tbl_34, tbl_35, tbl_36, tbl_37, tbl_38, tbl_39, W_top1, b_top1, W_top2, b_top2, W_top3, L0_rec_W):
    import jax
    import jax.numpy as jnp

    def _L0_rec_ref(embeddings, W):
        import jax, jax.numpy as jnp
        import numpy as np
        NUM_FIELDS = 40
        _I_IDX, _J_IDX = np.triu_indices(NUM_FIELDS, k=1)
        vi = embeddings[:, _I_IDX, :]
        vj = embeddings[:, _J_IDX, :]
        return jnp.einsum('bke,kef,bkf->bk', vi, W, vj)
    e = jnp.stack([tbl_0[ids[:, 0]], tbl_1[ids[:, 1]], tbl_2[ids[:, 2]], tbl_3[ids[:, 3]], tbl_4[ids[:, 4]], tbl_5[ids[:, 5]], tbl_6[ids[:, 6]], tbl_7[ids[:, 7]], tbl_8[ids[:, 8]], tbl_9[ids[:, 9]], tbl_10[ids[:, 10]], tbl_11[ids[:, 11]], tbl_12[ids[:, 12]], tbl_13[ids[:, 13]], tbl_14[ids[:, 14]], tbl_15[ids[:, 15]], tbl_16[ids[:, 16]], tbl_17[ids[:, 17]], tbl_18[ids[:, 18]], tbl_19[ids[:, 19]], tbl_20[ids[:, 20]], tbl_21[ids[:, 21]], tbl_22[ids[:, 22]], tbl_23[ids[:, 23]], tbl_24[ids[:, 24]], tbl_25[ids[:, 25]], tbl_26[ids[:, 26]], tbl_27[ids[:, 27]], tbl_28[ids[:, 28]], tbl_29[ids[:, 29]], tbl_30[ids[:, 30]], tbl_31[ids[:, 31]], tbl_32[ids[:, 32]], tbl_33[ids[:, 33]], tbl_34[ids[:, 34]], tbl_35[ids[:, 35]], tbl_36[ids[:, 36]], tbl_37[ids[:, 37]], tbl_38[ids[:, 38]], tbl_39[ids[:, 39]]], axis=1)
    z = _L0_rec_ref(e, L0_rec_W)
    z = z.reshape(z.shape[0], -1)
    h = jnp.concatenate([z, dense_ctx], axis=1)
    h = jnp.maximum(h @ W_top1 + b_top1, 0.0)
    h = jnp.maximum(h @ W_top2 + b_top2, 0.0)
    y = h @ W_top3
    return y

_drawn_inputs = setup_inputs


def setup_inputs(seed=0):
    import zlib

    import numpy as np

    out = dict(_drawn_inputs(seed))
    spreads = {'b_top1': (0.0, 0.1), 'b_top2': (0.0, 0.1)}
    factors = {}
    for name, (base, spread) in spreads.items():
        noise = np.random.default_rng([zlib.crc32(name.encode()), seed]).standard_normal(out[name].shape)
        drawn = base * np.exp(spread * noise) if base else spread * noise
        out[name] = jnp.asarray(drawn.astype(out[name].dtype))
    for name, factor in factors.items():
        out[name] = (out[name] * factor).astype(out[name].dtype)
    return out
```

```python
import numpy as np
import concourse.bass as bass
from concourse import mybir
from contextlib import ExitStack

FP32 = mybir.dt.float32
FP32R = mybir.dt.float32r
INT32 = mybir.dt.int32
ALU = mybir.AluOpType
ACT = mybir.ActivationFunctionType

P = 128
BATCH, FIELDS, DIM = 2048, 40, 32
DENSE, HID1, HID2 = 16, 512, 256
PAIRS = FIELDS * (FIELDS - 1) // 2
HALVES = 2
TB = HALVES * P
TILES = BATCH // TB
PER = P // DIM
STAGES = FIELDS // PER
LEFTS = FIELDS - 1
PIECE = STAGES

GROUPS = [(c, m) for c in range(STAGES) for m in range(c + 1)]
NG = len(GROUPS)
GROUPS_BEFORE = [c * (c + 1) // 2 for c in range(STAGES + 1)]
Z_SLOTS = P // (PER * PER)
Z_BLOCKS = -(-NG // Z_SLOTS)

GATHER_SLOTS = 5
USES = STAGES // GATHER_SLOTS
SCRATCH = 4096
AUX_SLOTS = 2


def lefts(c, m):
    return [i for i in range(PER * m, PER * m + PER) if i < PER * c + PER - 1]


def first_stage(i):
    return (i + 1) // PER


def chunk_at(i, c):
    return sum(STAGES - first_stage(x) for x in range(i)) + c - first_stage(i)


CHUNKS = chunk_at(LEFTS - 1, STAGES - 1) + 1


def pair(i, j):
    return i * FIELDS - i * (i + 1) // 2 + j - i - 1


def jobs_of(first):
    jobs = {k: [] for k in range(-1, NG)}
    if not first:
        jobs[-1] = [("hid1", 0, 0), ("hid1", 0, 1)]
        jobs[2] = [("hid1", 1, 0), ("hid1", 1, 1)]
        jobs[4] = [("hid1", 2, 0)]
        jobs[5] = [("hid1", 2, 1)]
        jobs[7] = [("hid1", 3, 0)]
        jobs[8] = [("hid1", 3, 1)]
        jobs[9] = [("hid2", 0, 0), ("hid2", 1, 0)]
        jobs[10] = [("out", 0, 0)]
    for c in range(STAGES):
        at = -1 if c == 0 else GROUPS_BEFORE[c - 1]
        jobs[at] += [("stack", PER * c, 2), ("stack", PER * c + 2, min(2, LEFTS - PER * c - 2)),
                     ("right", c, 0)]
    return jobs


def fills(job):
    return not (job[0] == "hid1" and job[2] == 0)


def numbered(jobs):
    at, out = 0, {}
    for job in jobs:
        out[job] = at
        at += fills(job)
    return out, at


JOBS = {first: jobs_of(first) for first in (True, False)}
AUX, AUX_COUNT = {}, {}
for _first in (True, False):
    AUX[_first], AUX_COUNT[_first] = numbered([j for k in range(-1, NG) for j in JOBS[_first][k]])
AUX_TILE = AUX_COUNT[False]
AUX_MISSING = AUX_TILE - AUX_COUNT[True]
LAST_JOBS = [j for k in range(-1, NG) for j in JOBS[False][k] if j[0] in ("hid1", "hid2", "out")]
MLP_AREAS = sum(fills(j) for j in LAST_JOBS)
last_job = ("right", STAGES - 1, 0)


def aux_count(n, first, job):
    if first:
        return AUX[True][job] + 1
    return n * AUX_TILE + AUX[False][job] + 1 - AUX_MISSING


def aux_count_before(n, job):
    return n * AUX_TILE + AUX[False][job] + 1 - AUX_MISSING - AUX_TILE


def z_rows():
    rows = np.full((P, Z_BLOCKS), PAIRS + DENSE, np.int32)
    for k, (c, m) in enumerate(GROUPS):
        for i in lefts(c, m):
            for s in range(PER):
                if PER * c + s > i:
                    rows[P // PER * (i % PER) + PER * (k % Z_SLOTS) + s, k // Z_SLOTS] = pair(i, PER * c + s)
    for d in range(DENSE):
        rows[P // PER * (d // PER) + PER * (Z_SLOTS - 1) + d % PER, Z_BLOCKS - 1] = PAIRS + d
    return rows


def constants():
    ones = np.zeros((P, Z_SLOTS, P // PER), np.float32)
    for p in range(P):
        for r in range(Z_SLOTS):
            ones[p, r, PER * r + p // DIM] = 1.0
    keep_lo = np.where(np.arange(P) < P // 2, 0.0, -1.0).astype(np.float32)[:, None]
    return {"ident": np.eye(P, dtype=np.float32), "ones": ones, "keep_lo": keep_lo, "z_rows": z_rows()}


def dlrm_tower_kernel(nc, ids, tables, dense, w_pairs, w_top1, b_top1, w_top2, b_top2, w_top3,
                      ident_in, ones_in, keep_lo_in, z_rows_in, out):
    ids_v = ids.rearrange("(t h p) f -> p t h f", p=P, h=HALVES)
    dense_v = dense.rearrange("(t h p) (a d) -> t h p a d", p=P, h=HALVES, a=PER)
    out_v = out.rearrange("(t b) o -> t o b", b=TB)
    w_v = w_pairs.rearrange("k e f -> e k f")

    ctx = ExitStack()
    with ctx:
        def sb(name, shape, dt=FP32):
            return ctx.enter_context(nc.sbuf_tensor(name, shape, dt))

        def pb(name, shape):
            return ctx.enter_context(nc.psum_tensor(name, shape, FP32))

        def sem(name):
            return ctx.enter_context(nc.semaphore(name))

        w_split = sb("w_split", [P, CHUNKS, P], FP32R)
        w1 = sb("w1", [P, Z_BLOCKS, HID1])
        w2 = sb("w2", [P, HID1 // P, HID2])
        w3 = sb("w3", [P, HID2 // P])
        b1 = sb("b1", [P, HID1 // P])
        b2 = sb("b2", [P, HID2 // P])
        ident = sb("ident_sb", [P, P])
        ones = sb("ones_sb", [P, Z_SLOTS, P // PER])
        keep_lo = sb("keep_lo_sb", [P, 1])
        rows_sb = sb("rows_sb", [P, Z_BLOCKS], INT32)
        ids_all = sb("ids_all", [P, TILES, HALVES, FIELDS], INT32)
        w_raw = sb("w_raw", [P, 2, PIECE * P])
        w_hi = sb("w_hi", [P, PIECE * P], FP32R)
        ids_now = sb("ids_now", [P, HALVES, FIELDS], INT32)
        rows = sb("rows", [P, GATHER_SLOTS, HALVES, PER * DIM])
        hilo = sb("hilo", [P, 2, HALVES * PER, 2, 2, DIM], FP32R)
        stack = sb("stack", [P, LEFTS, TB], FP32R)
        right = sb("right", [P, 2, TB])
        prod = sb("prod", [P, 2, PER, TB])
        dense_pad = sb("dense_pad", [P, HALVES, PER, P // PER])
        z = sb("z", [P, Z_BLOCKS, TB])
        h1 = sb("h1", [P, HID1 // P, TB])
        h2 = sb("h2", [P, HID2 // P, TB])
        y = sb("y", [1, TB])

        t_ps = [pb(f"t_ps{s}", [P, PER, TB]) for s in range(2)]
        z_ps = [pb(f"z_ps{s}", [P, 2, TB]) for s in range(2)]
        aux_ps = [pb(f"aux_ps{s}", [P, 2, TB]) for s in range(AUX_SLOTS)]

        ids_loaded = sem("ids_loaded")
        consts_loaded = sem("consts_loaded")
        mlp_loaded = sem("mlp_loaded")
        rows_loaded = sem("rows_loaded")
        w1_zeroed = sem("w1_zeroed")
        w1_loaded = sem("w1_loaded")
        dense_zeroed = sem("dense_zeroed")
        dense_loaded = sem("dense_loaded")
        raw_loaded = [sem(f"raw_loaded{s}") for s in range(2)]
        raw_copied = [sem(f"raw_copied{s}") for s in range(2)]
        w_rounded = sem("w_rounded")
        w_ready = sem("w_ready")
        ids_copied = sem("ids_copied")
        stages_begun = sem("stages_begun")
        gathered = [sem(f"gathered{s}") for s in range(GATHER_SLOTS)]
        hi_ready = sem("hi_ready")
        hilo_ready = sem("hilo_ready")
        aux_filled = sem("aux_filled")
        aux_emptied = sem("aux_emptied")
        t_ready = sem("t_ready")
        prod_ready = sem("prod_ready")
        prod_used = sem("prod_used")
        z_whole = sem("z_whole")
        z_emptied = sem("z_emptied")
        y_free = sem("y_free")
        y_stored = sem("y_stored")

        block = ctx.enter_context(nc.Block())

        CONSTS, MLP_LOADS = 3, 4
        GATHERS = PER * HALVES
        STAGE_INC = 16 * GATHERS

        def piece(i):
            return (STAGES - first_stage(i)) * P, (i + 1 - PER * first_stage(i)) * DIM

        def split_at(i):
            return w_split[:, chunk_at(i, first_stage(i)):chunk_at(i, STAGES - 1) + 1, :].rearrange(
                "p c x -> p (c x)")

        def pieces_after(c, m):
            new = [i for i in range(PER * c + PER - 1, PER * c + 2 * PER - 1) if i < LEFTS]
            return [i for x, i in enumerate(new) if x * (c + 1) // PER == m]

        @block.sync
        def _(sp):
            sp.dma_start(ids_all[:, :, :, :], ids_v).then_inc(ids_loaded, 16)

            def load_piece(i):
                cols, skip = piece(i)
                if i >= 2:
                    sp.wait_ge(w_ready, i - 1)
                sp.dma_start(
                    w_raw[0:DIM, i % 2, skip:cols].rearrange("e (k f) -> e k f", f=DIM),
                    w_v[:, pair(i, i + 1):pair(i, i + 1) + FIELDS - 1 - i, :],
                ).then_inc(raw_loaded[i % 2], 16)

            def copy_piece(i):
                cols, skip = piece(i)
                sp.wait_ge(raw_loaded[i % 2], 16 * (i // 2 + 1))
                for q in range(1, PER):
                    sp.dma_start(w_raw[q * DIM:(q + 1) * DIM, i % 2, skip:cols],
                                 w_raw[0:DIM, i % 2, skip:cols]).then_inc(raw_copied[i % 2], 16)

            def load_dense(n):
                for h in range(HALVES):
                    sp.dma_start(dense_pad[:, h, :, P // PER - PER:P // PER],
                                 dense_v[n, h]).then_inc(dense_loaded, 16)

            load_piece(0)
            for i in range(LEFTS):
                if i + 1 < LEFTS:
                    load_piece(i + 1)
                copy_piece(i)
            sp.wait_ge(dense_zeroed, 1)
            load_dense(0)
            with sp.Fori(1, TILES) as n:
                sp.wait_ge(z_whole, n)
                load_dense(n)
                sp.wait_ge(aux_emptied, aux_count(n, False, ("out", 0, 0)))
                sp.dma_start(out_v[n - 1], y[:, :]).then_inc(y_stored, 16)
                sp.wait_ge(y_stored, n * 16)
                sp.sem_inc(y_free, 1)
            sp.wait_ge(aux_emptied, aux_count(TILES - 1, False, last_job) + MLP_AREAS)
            sp.dma_start(out_v[TILES - 1], y[:, :]).then_inc(y_stored, 16)
            sp.wait_ge(y_stored, 16 * TILES)

        @block.gpsimd
        def _(pool):
            pool.wait_ge(ids_loaded, 16)

            def copy_ids(n, lo):
                nc.gpsimd.tensor_copy(ids_now[:, :, lo:lo + FIELDS // 2],
                                      ids_all[:, n, :, lo:lo + FIELDS // 2]).then_inc(ids_copied, 1)
                pool.wait_ge(ids_copied, n * 2 + (1 if lo == 0 else 2))

            def tile(n, first):
                for c in range(STAGES):
                    slot = c % GATHER_SLOTS
                    if c >= GATHER_SLOTS:
                        pool.wait_ge(aux_filled, aux_count(n, first, ("right", c - GATHER_SLOTS, 0)))
                    elif not first:
                        pool.wait_ge(aux_filled, aux_count_before(n, ("right", c + GATHER_SLOTS, 0)))
                    if c == 0:
                        if not first:
                            for s in range(GATHER_SLOTS):
                                pool.wait_ge(gathered[s], n * STAGE_INC * USES - STAGE_INC)
                        copy_ids(n, 0)
                    if c == 2:
                        if not first:
                            for s in range(2, GATHER_SLOTS):
                                pool.wait_ge(gathered[s], n * STAGE_INC * USES)
                            for s in range(2):
                                pool.wait_ge(gathered[s], n * STAGE_INC * USES + STAGE_INC)
                        copy_ids(n, FIELDS // 2)
                    pool.sem_inc(stages_begun, 1)
                    for f in range(PER):
                        for h in range(HALVES):
                            field = PER * c + f
                            nc.gpsimd.indirect_dma_start(
                                rows[:, slot, h, f * DIM:(f + 1) * DIM], None, tables[field],
                                bass.IndirectOffsetOnAxis(ap=ids_now[:, h, field:field + 1], axis=0),
                            ).then_inc(gathered[slot], 16)
                    if first and c == GATHER_SLOTS - 1:
                        pool.wait_ge(rows_loaded, 16)
                        pool.wait_ge(w1_zeroed, 1)
                        for t in range(Z_BLOCKS):
                            nc.gpsimd.indirect_dma_start(
                                w1[:, t, :], None, w_top1,
                                bass.IndirectOffsetOnAxis(ap=rows_sb[:, t:t + 1], axis=0),
                                bounds_check=PAIRS + DENSE - 1, oob_is_err=False,
                            ).then_inc(w1_loaded, 16)

            tile(0, True)
            with pool.Fori(1, TILES) as n:
                tile(n, False)

        @block.scalar
        def _(act):
            act.dma_start(ident[:, :], ident_in).then_inc(consts_loaded, 16)
            act.dma_start(keep_lo[:, :], keep_lo_in).then_inc(consts_loaded, 16)
            act.dma_start(ones[:, :, :], ones_in).then_inc(consts_loaded, 16)
            act.dma_start(rows_sb[:, :], z_rows_in).then_inc(rows_loaded, 16)

            def load_mlp():
                act.dma_start(w2[:, :, :], w_top2.rearrange("(t p) n -> p t n", p=P)).then_inc(mlp_loaded, 16)
                with nc.allow_non_contiguous_dma(reason="a few columns of 128 values"):
                    act.dma_start(w3[:, :], w_top3.rearrange("(t p) o -> p (t o)", p=P)).then_inc(mlp_loaded, 16)
                    act.dma_start(b1[:, :], b_top1.rearrange("(t p) -> p t", p=P)).then_inc(mlp_loaded, 16)
                    act.dma_start(b2[:, :], b_top2.rearrange("(t p) -> p t", p=P)).then_inc(mlp_loaded, 16)

            def round_piece(i):
                cols, skip = piece(i)
                act.wait_ge(raw_copied[i % 2], 16 * (PER - 1) * (i // 2 + 1))
                if i >= 1:
                    act.wait_ge(w_ready, i)
                nc.scalar.activation(w_hi[:, skip:cols], w_raw[:, i % 2, skip:cols],
                                     ACT.Copy).then_inc(w_rounded, 1)

            def hi_part(n, first, c):
                act.wait_ge(gathered[c % GATHER_SLOTS],
                            n * STAGE_INC * USES + STAGE_INC * (c // GATHER_SLOTS + 1))
                if c >= 2:
                    act.wait_ge(aux_filled, aux_count(n, first, ("right", c - 2, 0)))
                elif not first:
                    act.wait_ge(aux_filled, aux_count_before(n, ("right", c - 2 + STAGES, 0)))
                src = rows[:, c % GATHER_SLOTS].rearrange("p h (f e) -> p (h f) e", e=DIM)
                nc.scalar.activation(hilo[:, c % 2, :, :, 0, :],
                                     src.unsqueeze(2).to_broadcast([P, HALVES * PER, 2, DIM]),
                                     ACT.Copy).then_inc(hi_ready, 1)

            def empty(n, first, job):
                kind, x, count = job
                act.wait_ge(aux_filled, aux_count(n, first, job))
                area = aux_ps[AUX[first][job] % AUX_SLOTS][:, 0, :]
                if kind == "stack":
                    nc.scalar.activation(stack[:, x:x + count, :],
                                         aux_ps[AUX[first][job] % AUX_SLOTS][:, 0:count, :],
                                         ACT.Copy).then_inc(aux_emptied, 1)
                elif kind == "right":
                    if x >= 2:
                        act.wait_ge(prod_ready, n * NG + GROUPS_BEFORE[x - 1])
                    elif not first:
                        act.wait_ge(prod_ready, n * NG + GROUPS_BEFORE[x - 1 + STAGES] - NG)
                    nc.scalar.activation(right[:, x % 2, :], area, ACT.Copy).then_inc(aux_emptied, 1)
                elif kind == "hid1":
                    nc.scalar.activation(h1[:, x, :], area, ACT.Relu,
                                         bias=b1[:, x:x + 1]).then_inc(aux_emptied, 1)
                elif kind == "hid2":
                    nc.scalar.activation(h2[:, x, :], area, ACT.Relu,
                                         bias=b2[:, x:x + 1]).then_inc(aux_emptied, 1)
                elif kind == "out":
                    act.wait_ge(y_free, n)
                    nc.scalar.activation(y[:, :], area[0:1, :], ACT.Copy).then_inc(aux_emptied, 1)

            def empty_z(n, first, t):
                if t < Z_BLOCKS - 1:
                    act.wait_ge(prod_used, n * NG + Z_SLOTS * (t + 1))
                else:
                    act.wait_ge(z_whole, n + 1)
                if not first:
                    act.wait_ge(aux_filled, aux_count(n, first, ("hid1", HID1 // P - 1, 1)))
                nc.scalar.activation(z[:, t, :], z_ps[t % 2][:, 0, :], ACT.Copy).then_inc(z_emptied, 1)

            def tile(n, first):
                hi_part(n, first, 0)
                for k in range(-1, NG):
                    if k >= 0:
                        c, m = GROUPS[k]
                        if m == 0 and c + 1 < STAGES:
                            hi_part(n, first, c + 1)
                    for job in JOBS[first][k]:
                        if fills(job):
                            empty(n, first, job)
                    if k > 0 and k % Z_SLOTS == 0:
                        empty_z(n, first, k // Z_SLOTS - 1)
                    if first and k >= 0:
                        for i in pieces_after(c, m):
                            round_piece(i)
                empty_z(n, first, Z_BLOCKS - 1)

            for i in range(PER - 1):
                round_piece(i)
            load_mlp()
            tile(0, True)
            act.wait_ge(mlp_loaded, 16 * MLP_LOADS)
            with act.Fori(1, TILES) as n:
                tile(n, False)
            for x, (kind, m, half) in enumerate([j for j in LAST_JOBS if fills(j)]):
                act.wait_ge(aux_filled, aux_count(TILES - 1, False, last_job) + x + 1)
                area = aux_ps[x % AUX_SLOTS][:, 0, :]
                if kind == "out":
                    act.wait_ge(y_free, TILES)
                    nc.scalar.activation(y[:, :], area[0:1, :], ACT.Copy).then_inc(aux_emptied, 1)
                else:
                    h, b = (h1, b1) if kind == "hid1" else (h2, b2)
                    nc.scalar.activation(h[:, m, :], area, ACT.Relu,
                                         bias=b[:, m:m + 1]).then_inc(aux_emptied, 1)

        @block.vector
        def _(dve):
            for i in range(LEFTS):
                if piece(i)[1]:
                    nc.vector.memset(split_at(i)[:, 0:piece(i)[1]].bitcast(FP32), 0.0)
            nc.vector.memset(dense_pad[:, :, :, :], 0.0).then_inc(dense_zeroed, 1)
            nc.vector.memset(y[:, :], 0.0).then_inc(y_free, 1)

            def split_piece(i):
                cols, skip = piece(i)
                dve.wait_ge(w_rounded, i + 1)
                nc.vector.scalar_tensor_tensor(
                    split_at(i)[:, skip:cols], w_hi[:, skip:cols].bitcast(FP32), keep_lo[:, 0:1],
                    w_raw[:, i % 2, skip:cols], ALU.mult, ALU.add).then_inc(w_ready, 1)

            def lo_part(n, c):
                dve.wait_ge(hi_ready, n * STAGES + c + 1)
                src = rows[:, c % GATHER_SLOTS].rearrange("p h (f e) -> p (h f) e", e=DIM)
                nc.vector.tensor_tensor(hilo[:, c % 2, :, :, 1, :],
                                        src.unsqueeze(2).to_broadcast([P, HALVES * PER, 2, DIM]),
                                        hilo[:, c % 2, :, :, 0, :].bitcast(FP32),
                                        ALU.subtract).then_inc(hilo_ready, 1)

            def tile(n, first):
                lo_part(n, 0)
                for k, (c, m) in enumerate(GROUPS):
                    if m == 0:
                        if c + 1 < STAGES:
                            lo_part(n, c + 1)
                        dve.wait_ge(aux_emptied, aux_count(n, first, ("right", c, 0)))
                    g = len(lefts(c, m))
                    dve.wait_ge(t_ready, n * NG + k + 1)
                    if k >= 2:
                        dve.wait_ge(prod_used, n * NG + k - 1)
                    elif not first:
                        dve.wait_ge(prod_used, n * NG)
                    nc.vector.tensor_tensor(
                        prod[:, k % 2, 0:g, :], t_ps[k % 2][:, 0:g, :],
                        right[:, c % 2, :].unsqueeze(1).to_broadcast([P, g, TB]),
                        ALU.mult).then_inc(prod_ready, 1)
                    if first:
                        for i in pieces_after(c, m):
                            split_piece(i)

            dve.wait_ge(consts_loaded, 16 * CONSTS)
            for i in range(PER - 1):
                split_piece(i)
            nc.vector.memset(w1[:, :, :], 0.0).then_inc(w1_zeroed, 1)
            tile(0, True)
            with dve.Fori(1, TILES) as n:
                tile(n, False)

        @block.tensor
        def _(pe):
            def stack_job(c):
                return [job for k in range(-1, NG) for job in JOBS[False][k]
                        if job[0] == "stack" and job[1] // PER == c][-1]

            def transform(n, first, k):
                c, m = GROUPS[k]
                if m == 0:
                    pe.wait_ge(aux_emptied, aux_count(n, first, stack_job(c)))
                    if first:
                        pe.wait_ge(w_ready, lefts(c, c)[-1] + 1)
                if k >= 2:
                    pe.wait_ge(prod_ready, n * NG + k - 1)
                elif not first:
                    pe.wait_ge(prod_ready, n * NG)
                for i in lefts(c, m):
                    last = nc.tensor.matmul(t_ps[k % 2][:, i % PER, :], w_split[:, chunk_at(i, c), :],
                                            stack[:, i, :], start=True, stop=True)
                last.then_inc(t_ready, 1)

            def sum_products(n, first, k):
                c, m = GROUPS[k]
                t, slot = divmod(k, Z_SLOTS)
                pe.wait_ge(prod_ready, n * NG + k + 1)
                if slot == 0:
                    if t >= 2:
                        pe.wait_ge(z_emptied, n * Z_BLOCKS + t - 1)
                    elif not first:
                        pe.wait_ge(z_emptied, n * Z_BLOCKS)
                in_block = range(Z_SLOTS * t, min(Z_SLOTS * t + Z_SLOTS, NG))
                for i in lefts(c, m):
                    a = i % PER
                    at = [x for x in in_block if len(lefts(*GROUPS[x])) > a]
                    last = nc.tensor.matmul(
                        z_ps[t % 2][a * DIM:(a + 1) * DIM, 0, :], ones[:, slot, :], prod[:, k % 2, a, :],
                        start=(k == at[0]), stop=(k == at[-1] and t < Z_BLOCKS - 1),
                        tile_position=(0, a * DIM))
                last.then_inc(prod_used, 1)
                if k == NG - 1:
                    add_dense(n)

            def add_dense(n):
                pe.wait_ge(dense_loaded, n * 16 * HALVES + 16 * HALVES)
                for h in range(HALVES):
                    for a in range(PER):
                        last = nc.tensor.matmul(
                            z_ps[(Z_BLOCKS - 1) % 2][a * DIM:(a + 1) * DIM, 0, h * P:(h + 1) * P],
                            dense_pad[:, h, a, :], ident[:, :], start=False, stop=(h == HALVES - 1),
                            tile_position=(0, a * DIM))
                last.then_inc(z_whole, 1)

            def mlp(kind, m, half, area):
                w, x, blocks = {"hid1": (w1, z, Z_BLOCKS), "hid2": (w2, h1, HID1 // P),
                                "out": (None, h2, HID2 // P)}[kind]
                part = range(blocks) if kind != "hid1" else (range(0, 4), range(4, blocks))[half]
                for t in part:
                    if kind == "out":
                        last = nc.tensor.matmul(area[0:1, :], w3[:, t:t + 1], x[:, t, :],
                                                start=(t == 0), stop=(t == blocks - 1))
                    else:
                        last = nc.tensor.matmul(area, w[:, t, m * P:(m + 1) * P], x[:, t, :],
                                                start=(t == 0), stop=(t == blocks - 1))
                return last

            def side_job(n, first, job):
                kind, x, half = job
                number = AUX[first][job]
                bank = aux_ps[number % AUX_SLOTS]
                if number >= AUX_SLOTS:
                    pe.wait_ge(aux_emptied, aux_count(n, first, job) - AUX_SLOTS)
                elif not first:
                    pe.wait_ge(aux_emptied, n * AUX_TILE - AUX_MISSING)
                if kind == "stack":
                    pe.wait_ge(hilo_ready, n * STAGES + x // PER + 1)
                    for d in range(half):
                        for h in range(HALVES):
                            src = hilo[:, x // PER % 2, h * PER + x % PER + d].rearrange("p r q e -> p (r q e)")
                            last = nc.tensor.transpose(bank[:, d, h * P:(h + 1) * P],
                                                       src.bitcast(FP32), ident[:, :])
                elif kind == "right":
                    pe.wait_ge(hilo_ready, n * STAGES + x + 1)
                    for h in range(HALVES):
                        last = nc.tensor.transpose(bank[:, 0, h * P:(h + 1) * P],
                                                   rows[:, x % GATHER_SLOTS, h, :], ident[:, :])
                else:
                    if kind == "hid1":
                        pe.wait_ge(z_emptied, n * Z_BLOCKS)
                    elif kind == "hid2":
                        pe.wait_ge(aux_emptied, aux_count(n, first, ("hid1", HID1 // P - 1, 1)))
                    else:
                        pe.wait_ge(aux_emptied, aux_count(n, first, ("hid2", HID2 // P - 1, 0)))
                    last = mlp(kind, x, half, bank[:, 0, :])
                if fills(job):
                    last.then_inc(aux_filled, 1)

            def tile(n, first):
                for job in JOBS[first][-1]:
                    side_job(n, first, job)
                for k in range(NG):
                    transform(n, first, k)
                    for job in JOBS[first][k]:
                        side_job(n, first, job)
                    if k:
                        sum_products(n, first, k - 1)
                sum_products(n, first, NG - 1)

            pe.wait_ge(consts_loaded, 16 * CONSTS)
            tile(0, True)
            pe.wait_ge(w1_loaded, 16 * Z_BLOCKS)
            pe.wait_ge(mlp_loaded, 16 * MLP_LOADS)
            with pe.Fori(1, TILES) as n:
                tile(n, False)
            done = aux_count(TILES - 1, False, last_job)
            pe.wait_ge(aux_emptied, done)
            pe.wait_ge(z_emptied, TILES * Z_BLOCKS)
            x = 0
            for kind, m, half in LAST_JOBS:
                if kind == "hid2":
                    pe.wait_ge(aux_emptied, done + HID1 // P)
                elif kind == "out":
                    pe.wait_ge(aux_emptied, done + HID1 // P + HID2 // P)
                if x >= AUX_SLOTS:
                    pe.wait_ge(aux_emptied, done + x - AUX_SLOTS + 1)
                last = mlp(kind, m, half, aux_ps[x % AUX_SLOTS][:, 0, :])
                if fills((kind, m, half)):
                    last.then_inc(aux_filled, 1)
                    x += 1


def kernel(**inputs):
    import concourse.bacc as bacc
    from concourse.bass_utils import run_bass_kernel_spmd

    nc = bacc.Bacc("TRN2", target_bir_lowering=False, num_devices=1, dynamic_dma_scratch_size=SCRATCH)
    names = ["ids"] + [f"tbl_{f}" for f in range(FIELDS)] + [
        "dense_ctx", "L0_rec_W", "W_top1", "b_top1", "W_top2", "b_top2", "W_top3"]
    arrays = {f"in_{name}": np.ascontiguousarray(inputs[name]) for name in names}
    arrays |= {f"const_{name}": a for name, a in constants().items()}
    args = [nc.dram_tensor(name, a.shape, mybir.dt.from_np(a.dtype), kind="ExternalInput").ap()
            for name, a in arrays.items()]
    out = nc.dram_tensor("out", (BATCH, 1), FP32, kind="ExternalOutput").ap()
    dlrm_tower_kernel(nc, args[0], args[1:1 + FIELDS], *args[1 + FIELDS:], out)
    r = run_bass_kernel_spmd(nc, [arrays], core_ids=[0])
    return r.results[0]["out"]
```

```python
import numpy as np
import concourse.bass as bass
from concourse import mybir
from contextlib import ExitStack

FP32 = mybir.dt.float32
FP32R = mybir.dt.float32r
INT32 = mybir.dt.int32
ALU = mybir.AluOpType
ACT = mybir.ActivationFunctionType

P = 128
BATCH, FIELDS, DIM = 2048, 40, 32
DENSE, HID1, HID2 = 16, 512, 256
PAIRS = FIELDS * (FIELDS - 1) // 2
HALVES = 2
TB = HALVES * P
TILES = BATCH // TB
PER = P // DIM
STAGES = FIELDS // PER
LEFTS = FIELDS - 1

GROUPS = [(c, m) for c in range(STAGES) for m in range(c + 1)]
NG = len(GROUPS)
GROUPS_BEFORE = [c * (c + 1) // 2 for c in range(STAGES + 1)]
Z_SLOTS = P // (PER * PER)
Z_BLOCKS = -(-NG // Z_SLOTS)

SCRATCH = 4096
TURNS = 3


def lefts(c, m):
    return [i for i in range(PER * m, PER * m + PER) if i < PER * c + PER - 1]


def first_stage(i):
    return (i + 1) // PER


def chunk_at(i, c):
    return sum(STAGES - first_stage(x) for x in range(i)) + c - first_stage(i)


CHUNKS = chunk_at(LEFTS - 1, STAGES - 1) + 1


def pair(i, j):
    return i * FIELDS - i * (i + 1) // 2 + j - i - 1


def new_lefts(c):
    return [i for i in range(PER * c - 1, PER * c + PER - 1) if i >= 0]


def jobs_of(first, last):
    jobs = {k: [] for k in range(NG)}
    for c in range(1, STAGES if last else STAGES + 1):
        for x in range(TURNS):
            m = min(c - 1, x + 1) if c < STAGES else STAGES - 1 - TURNS + x
            jobs[GROUPS_BEFORE[c - 1] + m].append(("turn", c, x))
    for t in range(Z_BLOCKS - 1):
        for m in range(HID1 // P):
            jobs[Z_SLOTS * (t + 1) + 2 + m].append(("hid1", t, m))
    if not first:
        jobs[0] = [("hid1", Z_BLOCKS - 1, m) for m in range(HID1 // P)] + jobs[0]
        for k, job in ((14, ("hid2", 0, 0)), (15, ("hid2", 0, 1)), (19, ("hid2", 1, 0)),
                       (20, ("hid2", 1, 1)), (25, ("out", 0, 0))):
            jobs[k].append(job)
    return jobs


JOBS = {(first, last): jobs_of(first, last) for first, last in ((True, False), (False, False), (False, True))}
TAIL = HID2 // P + 1


def z_rows():
    rows = np.full((P, Z_BLOCKS), PAIRS + DENSE, np.int32)
    for k, (c, m) in enumerate(GROUPS):
        for i in lefts(c, m):
            for s in range(PER):
                if PER * c + s > i:
                    rows[P // PER * (i % PER) + PER * (k % Z_SLOTS) + s, k // Z_SLOTS] = pair(i, PER * c + s)
    for d in range(DENSE):
        rows[P // PER * (d // PER) + PER * (Z_SLOTS - 1) + d % PER, Z_BLOCKS - 1] = PAIRS + d
    return rows


def constants():
    ones = np.zeros((P, Z_SLOTS, P // PER), np.float32)
    for p in range(P):
        for r in range(Z_SLOTS):
            ones[p, r, PER * r + p // DIM] = 1.0
    return {"ident": np.eye(P, dtype=np.float32), "ones": ones, "z_rows": z_rows()}


def dlrm_tower_kernel(nc, ids, tables, dense, w_pairs, w_top1, b_top1, w_top2, b_top2, w_top3,
                      ident_in, ones_in, z_rows_in, out):
    ids_v = ids.rearrange("(t h p) f -> p t h f", p=P, h=HALVES)
    dense_v = dense.rearrange("(t h p) (a d) -> t h p a d", p=P, h=HALVES, a=PER)
    out_v = out.rearrange("(t b) o -> t o b", b=TB)
    w_v = w_pairs.rearrange("k e f -> e k f")

    ctx = ExitStack()
    with ctx:
        def sb(name, shape, dt=FP32):
            return ctx.enter_context(nc.sbuf_tensor(name, shape, dt))

        def pb(name, shape):
            return ctx.enter_context(nc.psum_tensor(name, shape, FP32))

        def sem(name):
            return ctx.enter_context(nc.semaphore(name))

        w_split = sb("w_split", [P, CHUNKS, P], FP32R)
        w1 = sb("w1", [P, Z_BLOCKS, HID1])
        w2 = sb("w2", [P, HID1 // P, HID2])
        w3 = sb("w3", [P, HID2 // P])
        b1 = sb("b1", [P, HID1 // P])
        b2 = sb("b2", [P, HID2 // P])
        ident = sb("ident_sb", [P, P])
        ones = sb("ones_sb", [P, Z_SLOTS, P // PER])
        rows_sb = sb("rows_sb", [P, Z_BLOCKS], INT32)
        ids_all = sb("ids_all", [P, TILES, HALVES, FIELDS], INT32)
        w_raw = sb("w_raw", [P, 2, STAGES * P])
        w_hi = sb("w_hi", [P, 2, STAGES * P], FP32R)
        ids_now = sb("ids_now", [P, HALVES, FIELDS], INT32)
        rows = sb("rows", [P, STAGES, HALVES, PER * DIM])
        hilo = sb("hilo", [P, 2, HALVES * PER, 2, 2, DIM], FP32R)
        stack = sb("stack", [P, LEFTS, TB], FP32R)
        right = sb("right", [P, 2, TB])
        prod = sb("prod", [P, 2, PER, TB])
        dense_pad = sb("dense_pad", [P, HALVES, PER, P // PER])
        z = sb("z", [P, 2, TB])
        h1 = w_raw[:, 0, 0:HID1 // P * TB].rearrange("p (m b) -> p m b", b=TB)
        h2 = w_raw[:, 1, 0:HID2 // P * TB].rearrange("p (m b) -> p m b", b=TB)
        y = sb("y", [1, TB])

        t_ps = [pb(f"t_ps{s}", [P, PER, TB]) for s in range(2)]
        z_ps = pb("z_ps", [P, 2, TB])
        h1_ps = pb("h1_ps", [P, HID1 // P, TB])
        aux_ps = pb("aux_ps", [P, 2, TB])

        ids_loaded = sem("ids_loaded")
        consts_loaded = sem("consts_loaded")
        mlp_loaded = sem("mlp_loaded")
        rows_loaded = sem("rows_loaded")
        w1_zeroed = sem("w1_zeroed")
        w1_loaded = sem("w1_loaded")
        raw_zeroed = sem("raw_zeroed")
        dense_zeroed = sem("dense_zeroed")
        dense_loaded = sem("dense_loaded")
        raw_loaded = [sem(f"raw_loaded{s}") for s in range(2)]
        lo_placed = [sem(f"lo_placed{s}") for s in range(2)]
        hi_placed = [sem(f"hi_placed{s}") for s in range(2)]
        w_hi_made = sem("w_hi_made")
        w_lo_made = sem("w_lo_made")
        ids_copied = sem("ids_copied")
        stages_begun = sem("stages_begun")
        gathered = [sem(f"gathered{c}") for c in range(STAGES)]
        hi_ready = sem("hi_ready")
        hilo_ready = sem("hilo_ready")
        turned = sem("turned")
        turn_taken = sem("turn_taken")
        t_ready = sem("t_ready")
        prod_ready = sem("prod_ready")
        prod_used = sem("prod_used")
        z_whole = sem("z_whole")
        z_taken = sem("z_taken")
        z_used = sem("z_used")
        h1_taken = sem("h1_taken")
        tail_filled = sem("tail_filled")
        tail_taken = sem("tail_taken")
        y_free = sem("y_free")
        y_stored = sem("y_stored")

        block = ctx.enter_context(nc.Block())

        CONSTS, MLP_LOADS = 2, 4
        STAGE_INC = 16 * PER * HALVES
        STAGE_TURNS = STAGES * TURNS

        def batch(c):
            for i in new_lefts(c):
                q = i + 1 - PER * c
                yield i, slice(q * DIM, (q + 1) * DIM), slice(q * DIM, (STAGES - c) * P)

        def placed(c):
            return sum(16 * 2 * len(new_lefts(x)) for x in range(c % 2, c + 1, 2))

        def split_at(i):
            return w_split[:, chunk_at(i, first_stage(i)):chunk_at(i, STAGES - 1) + 1, :].rearrange(
                "p c x -> p (c x)")

        @block.sync
        def _(sp):
            sp.dma_start(ids_all[:, :, :, :], ids_v).then_inc(ids_loaded, 16)

            def load_batch(c):
                if c >= 2:
                    sp.wait_ge(lo_placed[c % 2], placed(c - 2))
                for i, at, cols in batch(c):
                    sp.dma_start(
                        w_raw[at, c % 2, cols].rearrange("e (k f) -> e k f", f=DIM),
                        w_v[:, pair(i, i + 1):pair(i, i + 1) + FIELDS - 1 - i, :],
                    ).then_inc(raw_loaded[c % 2], 16)

            def place_batch(c):
                sp.wait_ge(w_lo_made, c + 1)
                for part, made, to in ((1, w_raw[:, :, :], lo_placed),
                                       (0, w_hi[:, :, :].bitcast(FP32), hi_placed)):
                    for i, at, cols in batch(c):
                        for q in (2 * part, 2 * part + 1):
                            sp.dma_start(split_at(i)[q * DIM:(q + 1) * DIM, cols].bitcast(FP32),
                                         made[at, c % 2, cols]).then_inc(to[c % 2], 16)

            def load_dense(n):
                for h in range(HALVES):
                    sp.dma_start(dense_pad[:, h, :, P // PER - PER:P // PER],
                                 dense_v[n, h]).then_inc(dense_loaded, 16)

            sp.wait_ge(raw_zeroed, 1)
            load_batch(0)
            load_batch(1)
            for c in range(STAGES):
                place_batch(c)
                if c + 2 < STAGES:
                    load_batch(c + 2)
                if c == 0:
                    sp.wait_ge(dense_zeroed, 1)
                    load_dense(0)
            with sp.Fori(1, TILES) as n:
                sp.wait_ge(z_whole, n)
                load_dense(n)
                sp.wait_ge(tail_taken, n * TAIL)
                sp.dma_start(out_v[n - 1], y[:, :]).then_inc(y_stored, 16)
                sp.wait_ge(y_stored, n * 16)
                sp.sem_inc(y_free, 1)
            sp.wait_ge(tail_taken, TILES * TAIL)
            sp.dma_start(out_v[TILES - 1], y[:, :]).then_inc(y_stored, 16)
            sp.wait_ge(y_stored, 16 * TILES)

        @block.gpsimd
        def _(pool):
            pool.wait_ge(ids_loaded, 16)

            def copy_ids(n, half):
                fields = slice(half * FIELDS // 2, (half + 1) * FIELDS // 2)
                nc.gpsimd.tensor_copy(ids_now[:, :, fields], ids_all[:, n, :, fields]).then_inc(ids_copied, 1)
                pool.wait_ge(ids_copied, n * 2 + half + 1)

            def tile(n, first):
                for c in range(STAGES):
                    if c in (0, 2):
                        half = c // 2
                        if not first:
                            for x in range(half * STAGES // 2, (half + 1) * STAGES // 2):
                                pool.wait_ge(gathered[x], n * STAGE_INC)
                        copy_ids(n, half)
                    if not first:
                        pool.wait_ge(turned, n * STAGE_TURNS + TURNS * (c + 1) - STAGE_TURNS)
                    pool.sem_inc(stages_begun, 1)
                    for f in range(PER):
                        for h in range(HALVES):
                            field = PER * c + f
                            nc.gpsimd.indirect_dma_start(
                                rows[:, c, h, f * DIM:(f + 1) * DIM], None, tables[field],
                                bass.IndirectOffsetOnAxis(ap=ids_now[:, h, field:field + 1], axis=0),
                            ).then_inc(gathered[c], 16)
                    if first and c == 2:
                        pool.wait_ge(rows_loaded, 16)
                        pool.wait_ge(w1_zeroed, 1)
                        for t in range(Z_BLOCKS):
                            nc.gpsimd.indirect_dma_start(
                                w1[:, t, :], None, w_top1,
                                bass.IndirectOffsetOnAxis(ap=rows_sb[:, t:t + 1], axis=0),
                                bounds_check=PAIRS + DENSE - 1, oob_is_err=False,
                            ).then_inc(w1_loaded, 16)

            tile(0, True)
            with pool.Fori(1, TILES) as n:
                tile(n, False)

        @block.scalar
        def _(act):
            act.dma_start(ident[:, :], ident_in).then_inc(consts_loaded, 16)
            act.dma_start(ones[:, :, :], ones_in).then_inc(consts_loaded, 16)
            act.dma_start(rows_sb[:, :], z_rows_in).then_inc(rows_loaded, 16)

            def load_mlp():
                act.dma_start(w2[:, :, :], w_top2.rearrange("(t p) n -> p t n", p=P)).then_inc(mlp_loaded, 16)
                with nc.allow_non_contiguous_dma(reason="a few columns of 128 values"):
                    act.dma_start(w3[:, :], w_top3.rearrange("(t p) o -> p (t o)", p=P)).then_inc(mlp_loaded, 16)
                    act.dma_start(b1[:, :], b_top1.rearrange("(t p) -> p t", p=P)).then_inc(mlp_loaded, 16)
                    act.dma_start(b2[:, :], b_top2.rearrange("(t p) -> p t", p=P)).then_inc(mlp_loaded, 16)

            def weights_hi(c):
                act.wait_ge(raw_loaded[c % 2], placed(c) // 2)
                if c >= 2:
                    act.wait_ge(hi_placed[c % 2], placed(c - 2))
                nc.scalar.activation(w_hi[:, c % 2, 0:(STAGES - c) * P], w_raw[:, c % 2, 0:(STAGES - c) * P],
                                     ACT.Copy).then_inc(w_hi_made, 1)

            def rows_hi(n, c, fresh):
                act.wait_ge(gathered[c % STAGES], n * STAGE_INC + STAGE_INC * (1 + c // STAGES))
                if not fresh:
                    act.wait_ge(turned, n * STAGE_TURNS + TURNS * (c - 1))
                src = rows[:, c % STAGES].rearrange("p h (f e) -> p (h f) e", e=DIM)
                nc.scalar.activation(hilo[:, c % 2, :, :, 0, :],
                                     src.unsqueeze(2).to_broadcast([P, HALVES * PER, 2, DIM]),
                                     ACT.Copy).then_inc(hi_ready, 1)

            def take_turn(n, c, x, fresh):
                act.wait_ge(turned, n * STAGE_TURNS + TURNS * c + x + 1)
                if x < TURNS - 1:
                    i = PER * (c % STAGES) + 2 * x
                    wide = min(2, LEFTS - i)
                    nc.scalar.activation(stack[:, i:i + wide, :], aux_ps[:, 0:wide, :],
                                         ACT.Copy).then_inc(turn_taken, 1)
                else:
                    if not fresh:
                        act.wait_ge(prod_ready, n * NG + (GROUPS_BEFORE[c - 1] if c else
                                                          GROUPS_BEFORE[STAGES - 1] - NG))
                    nc.scalar.activation(right[:, c % 2, :], aux_ps[:, 0, :],
                                         ACT.Copy).then_inc(turn_taken, 1)

            def take_z(n, first, t):
                if t < Z_BLOCKS - 1:
                    act.wait_ge(prod_used, n * NG + Z_SLOTS * (t + 1))
                else:
                    act.wait_ge(z_whole, n + 1)
                if t >= 2:
                    act.wait_ge(z_used, n * Z_BLOCKS + t - 1)
                elif not first:
                    act.wait_ge(z_used, n * Z_BLOCKS)
                nc.scalar.activation(z[:, t % 2, :], z_ps[:, 0, :], ACT.Copy).then_inc(z_taken, 1)

            def take_h1(n):
                act.wait_ge(z_used, n * Z_BLOCKS)
                for m in range(HID1 // P):
                    last = nc.scalar.activation(h1[:, m, :], h1_ps[:, m, :], ACT.Relu, bias=b1[:, m:m + 1])
                last.then_inc(h1_taken, 1)

            def take_tail(n, kind, m):
                act.wait_ge(tail_filled, n * TAIL + (m + 1 if kind == "hid2" else TAIL) - TAIL)
                if kind == "hid2":
                    nc.scalar.activation(h2[:, m, :], aux_ps[:, 0, :], ACT.Relu,
                                         bias=b2[:, m:m + 1]).then_inc(tail_taken, 1)
                else:
                    act.wait_ge(y_free, n)
                    nc.scalar.activation(y[:, :], aux_ps[0:1, 0, :], ACT.Copy).then_inc(tail_taken, 1)

            def tile(n, first, last):
                for k, (c, m) in enumerate(GROUPS):
                    if m == 0 and not (last and c == STAGES - 1):
                        rows_hi(n, c + 1, fresh=first and c == 0)
                    for kind, x, y_ in JOBS[first, last][k]:
                        if kind == "turn":
                            take_turn(n, x, y_, fresh=first and x == 1)
                        elif kind == "hid1" and x == Z_BLOCKS - 1 and y_ == HID1 // P - 1:
                            take_h1(n)
                        elif kind == "out" or (kind == "hid2" and y_ == 1):
                            take_tail(n, kind, x)
                    if k > 0 and k % Z_SLOTS == 0:
                        take_z(n, first, k // Z_SLOTS - 1)
                    if first and m == 0 and c + 2 < STAGES:
                        weights_hi(c + 2)
                take_z(n, first, Z_BLOCKS - 1)

            weights_hi(0)
            weights_hi(1)
            load_mlp()
            rows_hi(0, 0, fresh=True)
            for x in range(TURNS):
                take_turn(0, 0, x, fresh=True)
            tile(0, True, False)
            act.wait_ge(mlp_loaded, 16 * MLP_LOADS)
            with act.Fori(1, TILES - 1) as n:
                tile(n, False, False)
            tile(TILES - 1, False, True)
            take_h1(TILES)
            for kind, m in [("hid2", m) for m in range(HID2 // P)] + [("out", 0)]:
                take_tail(TILES, kind, m)

        @block.vector
        def _(dve):
            nc.vector.memset(w_raw[:, :, 0:P], 0.0)
            nc.vector.memset(w_raw[0:DIM, 0, P:STAGES * P], 0.0).then_inc(raw_zeroed, 1)
            for i in range(LEFTS):
                skip = (i + 1) % PER * DIM
                if skip:
                    nc.vector.memset(split_at(i)[:, 0:skip].bitcast(FP32), 0.0)
            nc.vector.memset(dense_pad[:, :, :, :], 0.0).then_inc(dense_zeroed, 1)
            nc.vector.memset(y[:, :], 0.0).then_inc(y_free, 1)

            def weights_lo(c):
                dve.wait_ge(w_hi_made, c + 1)
                cols = slice(0, (STAGES - c) * P)
                nc.vector.tensor_tensor(w_raw[:, c % 2, cols], w_raw[:, c % 2, cols],
                                        w_hi[:, c % 2, cols].bitcast(FP32),
                                        ALU.subtract).then_inc(w_lo_made, 1)

            def rows_lo(n, c):
                dve.wait_ge(hi_ready, n * STAGES + c + 1)
                src = rows[:, c % STAGES].rearrange("p h (f e) -> p (h f) e", e=DIM)
                nc.vector.tensor_tensor(hilo[:, c % 2, :, :, 1, :],
                                        src.unsqueeze(2).to_broadcast([P, HALVES * PER, 2, DIM]),
                                        hilo[:, c % 2, :, :, 0, :].bitcast(FP32),
                                        ALU.subtract).then_inc(hilo_ready, 1)

            def tile(n, first, last):
                for k, (c, m) in enumerate(GROUPS):
                    if m == 0:
                        dve.wait_ge(turn_taken, n * STAGE_TURNS + TURNS * (c + 1))
                    g = len(lefts(c, m))
                    dve.wait_ge(t_ready, n * NG + k + 1)
                    if k >= 2:
                        dve.wait_ge(prod_used, n * NG + k - 1)
                    elif not first:
                        dve.wait_ge(prod_used, n * NG)
                    nc.vector.tensor_tensor(
                        prod[:, k % 2, 0:g, :], t_ps[k % 2][:, 0:g, :],
                        right[:, c % 2, :].unsqueeze(1).to_broadcast([P, g, TB]),
                        ALU.mult).then_inc(prod_ready, 1)
                    if m == 0 and not (last and c == STAGES - 1):
                        rows_lo(n, c + 1)
                    if first and m == 0 and c + 2 < STAGES:
                        weights_lo(c + 2)

            weights_lo(0)
            weights_lo(1)
            nc.vector.memset(w1[:, :, :], 0.0).then_inc(w1_zeroed, 1)
            rows_lo(0, 0)
            tile(0, True, False)
            with dve.Fori(1, TILES - 1) as n:
                tile(n, False, False)
            tile(TILES - 1, False, True)

        @block.tensor
        def _(pe):
            def transform(n, first, k):
                c, m = GROUPS[k]
                if m == 0:
                    pe.wait_ge(turn_taken, n * STAGE_TURNS + TURNS * c + TURNS - 1)
                    if first:
                        pe.wait_ge(lo_placed[c % 2], placed(c))
                        pe.wait_ge(hi_placed[c % 2], placed(c))
                if k >= 2:
                    pe.wait_ge(prod_ready, n * NG + k - 1)
                elif not first:
                    pe.wait_ge(prod_ready, n * NG)
                for i in lefts(c, m):
                    last = nc.tensor.matmul(t_ps[k % 2][:, i % PER, :], w_split[:, chunk_at(i, c), :],
                                            stack[:, i, :], start=True, stop=True)
                last.then_inc(t_ready, 1)

            def sum_products(n, first, k):
                c, m = GROUPS[k]
                t, slot = divmod(k, Z_SLOTS)
                pe.wait_ge(prod_ready, n * NG + k + 1)
                if slot == 0 and not (first and t == 0):
                    pe.wait_ge(z_taken, n * Z_BLOCKS + t)
                in_block = range(Z_SLOTS * t, min(Z_SLOTS * t + Z_SLOTS, NG))
                for i in lefts(c, m):
                    a = i % PER
                    at = [x for x in in_block if len(lefts(*GROUPS[x])) > a]
                    last = nc.tensor.matmul(
                        z_ps[a * DIM:(a + 1) * DIM, 0, :], ones[:, slot, :], prod[:, k % 2, a, :],
                        start=(k == at[0]), stop=(k == at[-1] and t < Z_BLOCKS - 1),
                        tile_position=(0, a * DIM))
                last.then_inc(prod_used, 1)

            def add_dense(n):
                pe.wait_ge(dense_loaded, n * 16 * HALVES + 16 * HALVES)
                for h in range(HALVES):
                    for a in range(PER):
                        last = nc.tensor.matmul(
                            z_ps[a * DIM:(a + 1) * DIM, 0, h * P:(h + 1) * P],
                            dense_pad[:, h, a, :], ident[:, :], start=False, stop=(h == HALVES - 1),
                            tile_position=(0, a * DIM))
                last.then_inc(z_whole, 1)

            def turn(n, c, x):
                pe.wait_ge(hilo_ready, n * STAGES + c + 1)
                src_c, i = c % STAGES, PER * (c % STAGES) + 2 * x
                if x < TURNS - 1:
                    for d in range(min(2, LEFTS - i)):
                        for h in range(HALVES):
                            src = hilo[:, c % 2, h * PER + 2 * x + d].rearrange("p r q e -> p (r q e)")
                            last = nc.tensor.transpose(aux_ps[:, d, h * P:(h + 1) * P],
                                                       src.bitcast(FP32), ident[:, :])
                else:
                    for h in range(HALVES):
                        last = nc.tensor.transpose(aux_ps[:, 0, h * P:(h + 1) * P],
                                                   rows[:, src_c, h, :], ident[:, :])
                last.then_inc(turned, 1)

            def hid1(t, m):
                return nc.tensor.matmul(h1_ps[:, m, :], w1[:, t, m * P:(m + 1) * P], z[:, t % 2, :],
                                        start=(t == 0 and m % 2 == 0), stop=(t == Z_BLOCKS - 1),
                                        skip_group_check=True)

            def hid2(m, half):
                for t in (2 * half, 2 * half + 1):
                    last = nc.tensor.matmul(aux_ps[:, 0, :], w2[:, t, m * P:(m + 1) * P], h1[:, t, :],
                                            start=(t == 0), stop=(t == HID1 // P - 1))
                return last

            def out_row():
                for t in range(HID2 // P):
                    last = nc.tensor.matmul(aux_ps[0:1, 0, :], w3[:, t:t + 1], h2[:, t, :],
                                            start=(t == 0), stop=(t == HID2 // P - 1))
                return last

            def first_layer(n, first, t, m):
                if m == 0:
                    if first and t == 0:
                        pe.wait_ge(w1_loaded, 16 * Z_BLOCKS)
                    pe.wait_ge(z_taken, n * Z_BLOCKS + t + 1)
                    if t == 0 and not first:
                        pe.wait_ge(h1_taken, n)
                last = hid1(t, m)
                if m == HID1 // P - 1:
                    last.then_inc(z_used, 1)

            def tail(n, kind, m, half):
                if kind == "hid2":
                    if m == 0 and half == 0:
                        pe.wait_ge(h1_taken, n)
                    elif half == 0:
                        pe.wait_ge(tail_taken, n * TAIL + m - TAIL)
                    last = hid2(m, half)
                    if half == 1:
                        last.then_inc(tail_filled, 1)
                else:
                    pe.wait_ge(tail_taken, n * TAIL - 1)
                    out_row().then_inc(tail_filled, 1)

            def tile(n, first, last_tile):
                tail_before = False
                taken = 0
                for k, (c, m) in enumerate(GROUPS):
                    transform(n, first, k)
                    for kind, x, y_ in JOBS[first, last_tile][k]:
                        if kind == "turn":
                            pe.wait_ge(turn_taken, n * STAGE_TURNS + TURNS * x + y_)
                            if tail_before:
                                pe.wait_ge(tail_taken, n * TAIL + taken - TAIL)
                                tail_before = False
                            turn(n, x, y_)
                        elif kind == "hid1":
                            if x == Z_BLOCKS - 1:
                                pe.wait_ge(z_taken, n * Z_BLOCKS)
                                last = hid1(x, y_)
                                if y_ == HID1 // P - 1:
                                    last.then_inc(z_used, 1)
                            else:
                                first_layer(n, first, x, y_)
                        else:
                            if not tail_before:
                                turns = sum(j[0] == "turn" for kk in range(k + 1)
                                            for j in JOBS[first, last_tile][kk])
                                pe.wait_ge(turn_taken, n * STAGE_TURNS + TURNS + turns)
                            tail(n, kind, x, y_)
                            tail_before = True
                            taken = x + 1 if kind == "hid2" else TAIL
                    if k:
                        sum_products(n, first, k - 1)
                sum_products(n, first, NG - 1)
                add_dense(n)

            pe.wait_ge(consts_loaded, 16 * CONSTS)
            for x in range(TURNS):
                if x:
                    pe.wait_ge(turn_taken, x)
                turn(0, 0, x)
            tile(0, True, False)
            pe.wait_ge(mlp_loaded, 16 * MLP_LOADS)
            with pe.Fori(1, TILES - 1) as n:
                tile(n, False, False)
            tile(TILES - 1, False, True)
            pe.wait_ge(z_taken, TILES * Z_BLOCKS)
            for m in range(HID1 // P):
                last = hid1(Z_BLOCKS - 1, m)
            last.then_inc(z_used, 1)
            pe.wait_ge(turn_taken, TILES * STAGE_TURNS)
            for m in range(HID2 // P):
                for half in range(2):
                    tail(TILES, "hid2", m, half)
            tail(TILES, "out", 0, 0)


def kernel(**inputs):
    import concourse.bacc as bacc
    from concourse.bass_utils import run_bass_kernel_spmd

    nc = bacc.Bacc("TRN2", target_bir_lowering=False, num_devices=1, dynamic_dma_scratch_size=SCRATCH)
    names = ["ids"] + [f"tbl_{f}" for f in range(FIELDS)] + [
        "dense_ctx", "L0_rec_W", "W_top1", "b_top1", "W_top2", "b_top2", "W_top3"]
    arrays = {f"in_{name}": np.ascontiguousarray(inputs[name]) for name in names}
    arrays |= {f"const_{name}": a for name, a in constants().items()}
    args = [nc.dram_tensor(name, a.shape, mybir.dt.from_np(a.dtype), kind="ExternalInput").ap()
            for name, a in arrays.items()]
    out = nc.dram_tensor("out", (BATCH, 1), FP32, kind="ExternalOutput").ap()
    dlrm_tower_kernel(nc, args[0], args[1:1 + FIELDS], *args[1 + FIELDS:], out)
    r = run_bass_kernel_spmd(nc, [arrays], core_ids=[0])
    return r.results[0]["out"]
```

```python
import numpy as np
import concourse.bass as bass
from concourse import mybir
from contextlib import ExitStack

FP32 = mybir.dt.float32
FP32R = mybir.dt.float32r
INT32 = mybir.dt.int32
ALU = mybir.AluOpType
ACT = mybir.ActivationFunctionType

P = 128
BATCH, FIELDS, DIM = 2048, 40, 32
DENSE, HID1, HID2 = 16, 512, 256
PAIRS = FIELDS * (FIELDS - 1) // 2
HALVES = 2
TB = HALVES * P
TILES = BATCH // TB
PER = P // DIM
STAGES = FIELDS // PER
LEFTS = FIELDS - 1

GROUPS = [(c, m) for c in range(STAGES) for m in range(c + 1)]
NG = len(GROUPS)
GROUPS_BEFORE = [c * (c + 1) // 2 for c in range(STAGES + 1)]
Z_SLOTS = P // (PER * PER)
Z_BLOCKS = -(-NG // Z_SLOTS)

SCRATCH = 3072
PROD_SLOTS = 3
Z_RING = 4
COPY_BLOCKS = PER * PER + 2
EARLY_FROM = 16
TURNS = 3


def lefts(c, m):
    return [i for i in range(PER * m, PER * m + PER) if i < PER * c + PER - 1]


def first_stage(i):
    return (i + 1) // PER


def chunk_at(i, c):
    return sum(STAGES - first_stage(x) for x in range(i)) + c - first_stage(i)


CHUNKS = chunk_at(LEFTS - 1, STAGES - 1) + 1


def pair(i, j):
    return i * FIELDS - i * (i + 1) // 2 + j - i - 1


def new_lefts(c):
    return [i for i in range(PER * c - 1, PER * c + PER - 1) if i >= 0]


PE_BATCHES = 4
BATCH_ORDER = [0, 1, 4, 2, 5, 3, 6, 7, 8, 9]
PARTS_BEFORE = {0: 3}
PARTS_AFTER = {0: 6, 1: 7, 6: 8, 18: 9}
PARTS_AT = {2: 3, 6: 4, 11: 5, 17: 6, 24: 7, 32: 8, 41: 9, 44: STAGES, 48: STAGES + 1, 54: STAGES + 2}
TURNS_AT = {2: (0, 1, 2), 3: (3, 4, 5), 4: (7, 8, 9), 5: (12, 13, 14), 6: (18, 19, 20),
            7: (25, 26, 27), 8: (33, 34, 35), 9: (42, 43, 44), STAGES: (46, 47, 48), STAGES + 1: (50, 51, 52)}
TURNS_BEFORE = 2 * TURNS
HID1_AT = ((12, 13, 14, 17), (21, 22, 23, 24), (28, 29, 30, 31), (36, 37, 39, 41),
           (43, 45, 47, 48), (50, 52, 53, 54), (NG + 1, NG + 1, NG + 2, NG + 3))
HID2_AT = ((5, 5, 5, 5), (6, 6, 6, 6))
OUT_AT = (10, 11)


def slots(count, again):
    order = [k % count for k in range(again)]
    order.append(order[again + 1 - count])
    while len(order) < NG:
        order.append(next(x for x in range(count) if x not in order[len(order) - count + 1:]))
    return order


def last_in_slot(order):
    twice = order + order
    return [max(x for x in range(k + NG) if twice[x] == order[k]) - NG for k in range(NG)]


T_SLOT, PROD_SLOT = slots(2, 42), slots(PROD_SLOTS, 18)
T_LAST, PROD_LAST = last_in_slot(T_SLOT), last_in_slot(PROD_SLOT)


def pieces(c):
    width = STAGES - c
    parts = -(-width // PER)
    cuts = [width * x // parts for x in range(parts + 1)]
    return [(i, a, b - a) for i in new_lefts(c) for a, b in zip(cuts, cuts[1:])]


PIECES = [(c, *piece) for c in range(PE_BATCHES) for piece in pieces(c)]
PIECES_TO = [sum(x[0] <= c for x in PIECES) for c in range(PE_BATCHES)]


PIECE_BANK = [p % 6 if p < PIECES_TO[2] else p % 2 for p in range(len(PIECES))]
ON_ACT = [p % 2 == 0 or p >= PIECES_TO[2] for p in range(len(PIECES))]


def prologue():
    piece = iter(range(PIECES_TO[2]))

    def some(n):
        return [("piece", p, 0) for _, p in zip(range(n), piece)]

    steps = [("weights", 0, 0), ("weights", 1, 0)] + some(4) + [("weights", 4, 0)] + some(2)
    steps += [("rows", 0, 0)] + some(3)
    steps += [("turn", 0, 0)] + some(2) + [("turn", 0, 1), ("weights", 2, 0)] + some(2) + [("turn", 0, 2)]
    steps += some(2) + [("weights", 5, 0)] + some(2) + [("rows", 1, 0)] + some(4)
    steps += [("turn", 1, 0)] + some(3) + [("turn", 1, 1)] + some(3) + [("turn", 1, 2)] + some(2)
    steps += [("rows", 2, 0)]
    return steps


PROLOGUE = prologue()


def jobs_of(first, last):
    jobs = {k: [] for k in range(NG)}
    if first:
        for p in range(PIECES_TO[2], PIECES_TO[3]):
            jobs[(p - PIECES_TO[2]) * 3 // len(pieces(3))].append(("piece", p, 0))
    for c, groups in TURNS_AT.items():
        for x, k in enumerate(groups):
            if c < STAGES or not last:
                jobs[k].append(("turn", c, x))
    if not first:
        for t, groups in enumerate(HID1_AT):
            for m, k in enumerate(groups):
                if k >= NG:
                    jobs[k - NG].append(("hid1_before", t, m))
    for t, groups in enumerate(HID1_AT):
        for m, k in enumerate(groups):
            if k < NG:
                jobs[k].append(("hid1", t, m))
    if not first:
        for m, groups in enumerate(HID2_AT):
            for t, k in enumerate(groups):
                jobs[k].append(("hid2", m, t))
        for t, k in enumerate(OUT_AT):
            jobs[k].append(("out", 0, t))
    return jobs


JOBS = {(first, last): jobs_of(first, last) for first, last in ((True, False), (False, False), (False, True))}
TAIL = HID2 // P + 1


def z_rows():
    rows = np.full((P, Z_BLOCKS), PAIRS + DENSE, np.int32)
    for k, (c, m) in enumerate(GROUPS):
        for i in lefts(c, m):
            for s in range(PER):
                if PER * c + s > i:
                    rows[P // PER * (i % PER) + PER * (k % Z_SLOTS) + s, k // Z_SLOTS] = pair(i, PER * c + s)
    for d in range(DENSE):
        rows[P // PER * (d // PER) + PER * (Z_SLOTS - 1) + d % PER, Z_BLOCKS - 1] = PAIRS + d
    return rows


def constants():
    ones = np.zeros((P, Z_SLOTS, P // PER), np.float32)
    for p in range(P):
        for r in range(Z_SLOTS):
            ones[p, r, PER * r + p // DIM] = 1.0
    copy2 = np.zeros((PER, DIM, COPY_BLOCKS, DIM), np.float32)
    for f in range(PER):
        for e in range(DIM):
            copy2[f, e, PER * f + 2:PER * f + 4, e] = 1.0
    return {"ident": np.eye(P, dtype=np.float32), "ones": ones, "z_rows": z_rows(),
            "copy2": copy2.reshape(P, COPY_BLOCKS * DIM)}


def dlrm_tower_kernel(nc, ids, tables, dense, w_pairs, w_top1, b_top1, w_top2, b_top2, w_top3,
                      ident_in, ones_in, z_rows_in, copy2_in, out):
    ids_v = ids.rearrange("(t h p) f -> p t h f", p=P, h=HALVES)
    dense_v = dense.rearrange("(t h p) (a d) -> t h p a d", p=P, h=HALVES, a=PER)
    out_v = out.rearrange("(t b) o -> t o b", b=TB)
    w2_v = w_top2.rearrange("(t p) n -> p t n", p=P)
    w_v = w_pairs.rearrange("k e f -> e k f")

    ctx = ExitStack()
    with ctx:
        def sb(name, shape, dt=FP32):
            return ctx.enter_context(nc.sbuf_tensor(name, shape, dt))

        def pb(name, shape):
            return ctx.enter_context(nc.psum_tensor(name, shape, FP32))

        def sem(name):
            return ctx.enter_context(nc.semaphore(name))

        w_split = sb("w_split", [P, CHUNKS, P], FP32R)
        w1 = sb("w1", [P, Z_BLOCKS, HID1])
        w3 = sb("w3", [P, HID2 // P])
        b1 = sb("b1", [P, HID1 // P])
        b2 = sb("b2", [P, HID2 // P])
        ident_r = sb("ident_r", [P, P], FP32R)
        ident = ident_r[:, :].bitcast(FP32)
        ones = sb("ones_sb", [P, Z_SLOTS, P // PER])
        rows_sb = sb("rows_sb", [P, Z_BLOCKS], INT32)
        ids_all = sb("ids_all", [P, TILES, HALVES, FIELDS], INT32)
        wide = [(STAGES - c) * P for c in range(STAGES)]
        raw, lo = {}, {}
        with ExitStack() as early:
            early.enter_context(nc.sbuf_tensor("before_raw", [P, EARLY_FROM, TB], FP32))
            for c in range(PE_BATCHES):
                raw[c] = early.enter_context(nc.sbuf_tensor(f"w_raw{c}", [P, wide[c]], FP32))
            w_hi_odd = early.enter_context(nc.sbuf_tensor("w_hi_odd", [P, wide[1]], FP32R))
        with ExitStack() as early:
            early.enter_context(nc.sbuf_tensor("before_lo", [P, EARLY_FROM, TB], FP32))
            for c in range(PE_BATCHES):
                lo[c] = early.enter_context(nc.sbuf_tensor(f"w_lo{c}", [P, wide[c]], FP32R))
        stack = sb("stack", [P, LEFTS, TB], FP32R)
        w_raw = [sb(f"w_raw_slot{x}", [P, wide[PE_BATCHES + x]]) for x in range(2)]
        with nc.sbuf_tensor("w_hi_even", [P, wide[0]], FP32R) as w_hi_even:
            pass
        h2_y = sb("h2_y", [P, wide[0]])
        w_hi = [sb(f"w_hi_slot{x}", [P, wide[PE_BATCHES + x]], FP32R) for x in range(2)]
        hi = {c: (w_hi_odd if c % 2 else w_hi_even) for c in range(PE_BATCHES)}
        for c in range(PE_BATCHES, STAGES):
            raw[c], lo[c], hi[c] = w_raw[c % 2], w_raw[c % 2], w_hi[c % 2]
        ids_now = sb("ids_now", [P, HALVES, FIELDS], INT32)
        rows = sb("rows", [P, STAGES, HALVES, PER * DIM])
        hilo = sb("hilo", [P, 2, HALVES * PER, 2, 2, DIM], FP32R)
        right = sb("right", [P, 3, TB])
        prod = sb("prod", [P, PROD_SLOTS, PER, TB])
        dense_pad = sb("dense_pad", [P, HALVES, PER, P // PER])
        z = sb("z", [P, Z_RING, TB])
        with nc.sbuf_tensor("copy2_sb", [P, COPY_BLOCKS * DIM], FP32R) as copy2:
            pass
        h1 = sb("h1", [P, HID1 // P, TB])
        h2 = h2_y[:, 0:HID2 // P * TB].rearrange("p (m b) -> p m b", b=TB)
        y = h2_y[0:1, HID2 // P * TB:HID2 // P * TB + TB]
        w2 = [w_raw[x][:, 0:2 * HID2].rearrange("p (t n) -> p t n", n=HID2) for x in range(2)]
        copy2_raw = prod[:, 0, :, :].rearrange("p a b -> p (a b)")[:, 0:COPY_BLOCKS * DIM]
        ident_raw = prod[:, 1, 0, 0:P]

        t_ps = [pb(f"t_ps{s}", [P, PER, TB]) for s in range(2)]
        z_ps = pb("z_ps", [P, 2, TB])
        h1_ps = pb("h1_ps", [P, HID1 // P, TB])
        piece_ps = [bank[:, 2 * x:2 * x + 2, :].rearrange("p m b -> p (m b)")
                    for bank in (h1_ps, *t_ps) for x in range(2)]
        aux_ps = pb("aux_ps", [P, 2, TB])

        last_hid2_ps = [aux_ps[:, 0, :], t_ps[0][:, 0, :]]

        ids_loaded = sem("ids_loaded")
        consts_loaded = sem("consts_loaded")
        mlp_loaded = sem("mlp_loaded")
        rows_loaded = sem("rows_loaded")
        w1_zeroed = sem("w1_zeroed")
        w1_loaded = sem("w1_loaded")
        raw_zeroed = sem("raw_zeroed")
        dense_zeroed = sem("dense_zeroed")
        dense_loaded = sem("dense_loaded")
        placers_loaded = sem("placers_loaded")
        copy2_ready = sem("copy2_ready")
        raw_loaded = [sem(f"raw_loaded{c}") for c in range(PE_BATCHES + 2)]
        raw_loaded += [raw_loaded[PE_BATCHES + c % 2] for c in range(PE_BATCHES + 2, STAGES)]
        lo_placed = [sem(f"lo_placed{x}") for x in range(2)]
        hi_placed = [sem(f"hi_placed{x}") for x in range(2)]
        piece_filled = sem("piece_filled")
        piece_taken = sem("piece_taken")
        piece_taken_dve = sem("piece_taken_dve")
        w_hi_made = sem("w_hi_made")
        w_lo_made = sem("w_lo_made")
        ids_copied = sem("ids_copied")
        stages_begun = sem("stages_begun")
        gathered = [sem(f"gathered{c}") for c in range(STAGES)]
        hi_ready = sem("hi_ready")
        hilo_ready = sem("hilo_ready")
        turned = sem("turned")
        turn_taken = sem("turn_taken")
        t_ready = sem("t_ready")
        prod_ready = sem("prod_ready")
        prod_used = sem("prod_used")
        dense_used = sem("dense_used")
        z_taken = sem("z_taken")
        z_used = sem("z_used")
        h1_taken = sem("h1_taken")
        last_h1_summed = sem("last_h1_summed")
        last_h1_taken = sem("last_h1_taken")
        tail_filled = sem("tail_filled")
        tail_taken = sem("tail_taken")
        y_free = sem("y_free")
        y_stored = sem("y_stored")

        block = ctx.enter_context(nc.Block())

        MLP_LOADS = 5
        STAGE_INC = 16 * PER * HALVES
        STAGE_TURNS = STAGES * TURNS

        def wait_pieces(engine, upto):
            engine.wait_ge(piece_taken, sum(ON_ACT[:upto]))
            if not all(ON_ACT[:upto]):
                engine.wait_ge(piece_taken_dve, upto - sum(ON_ACT[:upto]))

        def piece_place(p):
            c, i, first, chunks = PIECES[p]
            at = chunk_at(i, c) + first
            return w_split[:, at:at + chunks, :].rearrange("p c x -> p (c x)")

        def piece_bank(p):
            return piece_ps[PIECE_BANK[p]][:, 0:PIECES[p][3] * P]

        def right_slot(c):
            return 2 if c % STAGES == 1 else c % STAGES % 2

        def right_before(c):
            return {1: GROUPS_BEFORE[2] - NG, 0: GROUPS_BEFORE[9] - NG, 3: 0}.get(
                c % STAGES, GROUPS_BEFORE[c % STAGES - 1]) + c // STAGES * NG

        def before(c):
            return [x for x in range(PE_BATCHES, c) if x % 2 == c % 2] if c > PE_BATCHES + 1 else []

        def batch(c):
            for i in new_lefts(c):
                q = i + 1 - PER * c
                yield i, q, slice(q * DIM, (q + 1) * DIM)

        def raw_loads(c):
            return sum(16 * len(new_lefts(x)) for x in before(c) + [c])

        def placed(c):
            return 2 * raw_loads(c)

        def made(c):
            return BATCH_ORDER.index(c) + 1

        @block.sync
        def _(sp):
            sp.dma_start(ids_all[:, :, :, :], ids_v).then_inc(ids_loaded, 16)

            def load_batch(c):
                for i, q, at in batch(c):
                    sp.dma_start(
                        raw[c][at, q * DIM:wide[c]].rearrange("e (k f) -> e k f", f=DIM),
                        w_v[:, pair(i, i + 1):pair(i, i + 1) + FIELDS - 1 - i, :],
                    ).then_inc(raw_loaded[c], 16)

            def place_batch(c):
                sp.wait_ge(w_lo_made, made(c))
                for part, of, to in ((1, lo[c][:, :], lo_placed),
                                     (0, hi[c][:, :].bitcast(FP32), hi_placed)):
                    for i, _, at in batch(c):
                        for q in (2 * part, 2 * part + 1):
                            sp.dma_start(w_split[q * DIM:(q + 1) * DIM, chunk_at(i, c):
                                                 chunk_at(i, STAGES - 1) + 1, :].bitcast(FP32),
                                         of[at, 0:wide[c]].rearrange("p (c x) -> p c x", x=P),
                                         ).then_inc(to[c % 2], 16)

            def load_dense(n):
                for h in range(HALVES):
                    sp.dma_start(dense_pad[:, h, :, P // PER - PER:P // PER],
                                 dense_v[n, h]).then_inc(dense_loaded, 16)

            sp.wait_ge(raw_zeroed, 1)
            load_batch(0)
            sp.wait_ge(raw_zeroed, 2)
            for c in BATCH_ORDER[1:PE_BATCHES + 2]:
                load_batch(c)
            sp.wait_ge(dense_zeroed, 1)
            load_dense(0)
            for c in range(PE_BATCHES, STAGES):
                place_batch(c)
                if c + 2 < STAGES:
                    sp.wait_ge(lo_placed[c % 2], placed(c))
                    load_batch(c + 2)
            for c in (STAGES - 2, STAGES - 1):
                sp.wait_ge(lo_placed[c % 2], placed(c))
                sp.dma_start(w2[c % 2], w2_v[:, 2 * (c % 2):2 * (c % 2) + 2, :]).then_inc(mlp_loaded, 16)
            with sp.Fori(1, TILES) as n:
                sp.wait_ge(dense_used, n)
                load_dense(n)
                sp.wait_ge(tail_taken, n * TAIL)
                sp.dma_start(out_v[n - 1], y).then_inc(y_stored, 16)
                sp.wait_ge(y_stored, n * 16)
                sp.sem_inc(y_free, 1)
            sp.wait_ge(tail_taken, TILES * TAIL)
            sp.dma_start(out_v[TILES - 1], y).then_inc(y_stored, 16)
            sp.wait_ge(y_stored, 16 * TILES)

        @block.gpsimd
        def _(pool):
            pool.wait_ge(ids_loaded, 16)

            def copy_ids(n, half):
                fields = slice(half * FIELDS // 2, (half + 1) * FIELDS // 2)
                nc.gpsimd.tensor_copy(ids_now[:, :, fields], ids_all[:, n, :, fields]).then_inc(ids_copied, 1)
                pool.wait_ge(ids_copied, n * 2 + half + 1)

            def tile(n, first):
                for c in range(STAGES):
                    if c in (0, 2):
                        half = c // 2
                        if not first:
                            for x in range(half * STAGES // 2, (half + 1) * STAGES // 2):
                                pool.wait_ge(gathered[x], n * STAGE_INC)
                        copy_ids(n, half)
                    if not first:
                        pool.wait_ge(turned, n * STAGE_TURNS + TURNS * (c + 1) - STAGE_TURNS)
                    pool.sem_inc(stages_begun, 1)
                    for f in range(PER):
                        for h in range(HALVES):
                            field = PER * c + f
                            nc.gpsimd.indirect_dma_start(
                                rows[:, c, h, f * DIM:(f + 1) * DIM], None, tables[field],
                                bass.IndirectOffsetOnAxis(ap=ids_now[:, h, field:field + 1], axis=0),
                            ).then_inc(gathered[c], 16)
                    if first and c == 2:
                        pool.wait_ge(rows_loaded, 16)
                        pool.wait_ge(w1_zeroed, 1)
                        for t in range(Z_BLOCKS):
                            nc.gpsimd.indirect_dma_start(
                                w1[:, t, :], None, w_top1,
                                bass.IndirectOffsetOnAxis(ap=rows_sb[:, t:t + 1], axis=0),
                                bounds_check=PAIRS + DENSE - 1, oob_is_err=False,
                            ).then_inc(w1_loaded, 16)

            tile(0, True)
            with pool.Fori(1, TILES) as n:
                tile(n, False)

        @block.scalar
        def _(act):
            act.dma_start(ident_raw, ident_in).then_inc(placers_loaded, 16)
            act.dma_start(ones[:, :, :], ones_in).then_inc(consts_loaded, 16)
            act.dma_start(copy2_raw, copy2_in).then_inc(placers_loaded, 16)
            act.dma_start(rows_sb[:, :], z_rows_in).then_inc(rows_loaded, 16)

            def load_mlp():
                with nc.allow_non_contiguous_dma(reason="a few columns of 128 values"):
                    act.dma_start(w3[:, :], w_top3.rearrange("(t p) o -> p (t o)", p=P)).then_inc(mlp_loaded, 16)
                    act.dma_start(b1[:, :], b_top1.rearrange("(t p) -> p t", p=P)).then_inc(mlp_loaded, 16)
                    act.dma_start(b2[:, :], b_top2.rearrange("(t p) -> p t", p=P)).then_inc(mlp_loaded, 16)

            def weights_hi(c):
                act.wait_ge(raw_loaded[c], raw_loads(c))
                if before(c):
                    act.wait_ge(hi_placed[c % 2], placed(before(c)[-1]))
                elif 2 <= c < PE_BATCHES:
                    act.wait_ge(piece_filled, PIECES_TO[c - 2])
                nc.scalar.activation(hi[c][:, 0:wide[c]], raw[c][:, 0:wide[c]], ACT.Copy).then_inc(w_hi_made, 1)

            def take_piece(p):
                act.wait_ge(piece_filled, p + 1)
                nc.scalar.activation(piece_place(p), piece_bank(p), ACT.Copy).then_inc(piece_taken, 1)

            def rows_hi(n, c, fresh):
                act.wait_ge(gathered[c % STAGES], n * STAGE_INC + STAGE_INC * (1 + c // STAGES))
                if not fresh:
                    act.wait_ge(turned, n * STAGE_TURNS + TURNS * (c - 1))
                src = rows[:, c % STAGES].rearrange("p h (f e) -> p (h f) e", e=DIM)
                nc.scalar.activation(hilo[:, c % 2, :, :, 0, :],
                                     src.unsqueeze(2).to_broadcast([P, HALVES * PER, 2, DIM]),
                                     ACT.Copy).then_inc(hi_ready, 1)

            def take_turn(n, c, x, fresh):
                act.wait_ge(turned, n * STAGE_TURNS + TURNS * c + x + 1)
                if x < TURNS - 1:
                    i = PER * (c % STAGES) + 2 * x
                    fields = min(2, LEFTS - i)
                    nc.scalar.activation(stack[:, i:i + fields, :], aux_ps[:, 0:fields, :],
                                         ACT.Copy).then_inc(turn_taken, 1)
                else:
                    if not fresh:
                        act.wait_ge(prod_ready, n * NG + right_before(c))
                    nc.scalar.activation(right[:, right_slot(c), :], aux_ps[:, 0, :],
                                         ACT.Copy).then_inc(turn_taken, 1)

            def take_z(n, first, t):
                act.wait_ge(prod_used, n * NG + min(Z_SLOTS * (t + 1), NG))
                if t >= Z_RING:
                    act.wait_ge(z_used, n * Z_BLOCKS + t + 1 - Z_RING)
                elif not first:
                    last = max(x for x in range(Z_BLOCKS) if x % Z_RING == t)
                    act.wait_ge(z_used, n * Z_BLOCKS + last + 1 - Z_BLOCKS)
                nc.scalar.activation(z[:, t % Z_RING, :], z_ps[:, 0, :], ACT.Copy).then_inc(z_taken, 1)

            def take_h1(n):
                act.wait_ge(z_used, n * Z_BLOCKS)
                for m in range(HID1 // P):
                    last = nc.scalar.activation(h1[:, m, :], h1_ps[:, m, :], ACT.Relu, bias=b1[:, m:m + 1])
                last.then_inc(h1_taken, 1)

            def take_tail(n, kind, m, of=aux_ps[:, 0, :]):
                act.wait_ge(tail_filled, n * TAIL + (m + 1 if kind == "hid2" else TAIL) - TAIL)
                if kind == "hid2":
                    nc.scalar.activation(h2[:, m, :], of, ACT.Relu,
                                         bias=b2[:, m:m + 1]).then_inc(tail_taken, 1)
                else:
                    act.wait_ge(y_free, n)
                    nc.scalar.activation(y, aux_ps[0:1, 0, :], ACT.Copy).then_inc(tail_taken, 1)

            def tile(n, first, last):
                if not first:
                    take_z(n - 1, False, Z_BLOCKS - 1)
                for k, (c, m) in enumerate(GROUPS):
                    if first and k in PARTS_BEFORE:
                        weights_hi(PARTS_BEFORE[k])
                    if k in PARTS_AT and not (last and PARTS_AT[k] >= STAGES):
                        rows_hi(n, PARTS_AT[k], fresh=False)
                    for kind, x, y_ in JOBS[first, last][k]:
                        if kind == "piece":
                            take_piece(x)
                        elif kind == "turn":
                            take_turn(n, x, y_, fresh=first and x == 3)
                        elif kind == "hid1_before" and x == Z_BLOCKS - 1 and y_ == HID1 // P - 1:
                            take_h1(n)
                        elif (kind == "hid2" and y_ == HID1 // P - 1) or (kind == "out" and y_ == HID2 // P - 1):
                            take_tail(n, kind, x)
                    if k > 0 and k % Z_SLOTS == 0:
                        take_z(n, first, k // Z_SLOTS - 1)
                    if first and k in PARTS_AFTER:
                        weights_hi(PARTS_AFTER[k])

            act.wait_ge(placers_loaded, 32)
            nc.scalar.activation(ident_r[:, :], ident_raw, ACT.Copy)
            nc.scalar.activation(copy2[:, :], copy2_raw, ACT.Copy).then_inc(copy2_ready, 1)
            for kind, x, y_ in PROLOGUE:
                if kind == "weights":
                    weights_hi(x)
                elif kind == "rows":
                    rows_hi(0, x, fresh=x < 2)
                elif kind == "piece":
                    if ON_ACT[x]:
                        take_piece(x)
                else:
                    take_turn(0, x, y_, fresh=x < 2)
            load_mlp()
            tile(0, True, False)
            act.wait_ge(mlp_loaded, 16 * MLP_LOADS)
            with act.Fori(1, TILES - 1) as n:
                tile(n, False, False)
            tile(TILES - 1, False, True)
            take_z(TILES - 1, False, Z_BLOCKS - 1)
            for m in range(HID1 // P):
                act.wait_ge(last_h1_summed, m // 2 + 1)
                last = nc.scalar.activation(h1[:, m, :], h1_ps[:, m, :], ACT.Relu, bias=b1[:, m:m + 1])
                if m % 2 == 1:
                    last.then_inc(last_h1_taken, 1)
            for m in range(HID2 // P):
                take_tail(TILES, "hid2", m, last_hid2_ps[m])
            take_tail(TILES, "out", 0)

        @block.vector
        def _(dve):
            nc.vector.memset(raw[0][0:DIM, P:wide[0]], 0.0)
            nc.vector.memset(raw[0][:, 0:P], 0.0).then_inc(raw_zeroed, 1)
            for c in range(1, PE_BATCHES + 2):
                last = nc.vector.memset(raw[c][:, 0:P], 0.0)
            last.then_inc(raw_zeroed, 1)
            nc.vector.memset(dense_pad[:, :, :, :], 0.0).then_inc(dense_zeroed, 1)
            nc.vector.memset(w1[:, :, :], 0.0).then_inc(w1_zeroed, 1)
            dve.sem_inc(y_free, 1)

            def weights_lo(c):
                dve.wait_ge(w_hi_made, made(c))
                nc.vector.tensor_tensor(lo[c][:, 0:wide[c]], raw[c][:, 0:wide[c]],
                                        hi[c][:, 0:wide[c]].bitcast(FP32), ALU.subtract).then_inc(w_lo_made, 1)

            def take_piece(p):
                dve.wait_ge(piece_filled, p + 1)
                nc.vector.tensor_copy(piece_place(p), piece_bank(p)).then_inc(piece_taken_dve, 1)

            def rows_lo(n, c):
                dve.wait_ge(hi_ready, n * STAGES + c + 1)
                src = rows[:, c % STAGES].rearrange("p h (f e) -> p (h f) e", e=DIM)
                nc.vector.tensor_tensor(hilo[:, c % 2, :, :, 1, :],
                                        src.unsqueeze(2).to_broadcast([P, HALVES * PER, 2, DIM]),
                                        hilo[:, c % 2, :, :, 0, :].bitcast(FP32),
                                        ALU.subtract).then_inc(hilo_ready, 1)

            def tile(n, first, last):
                for k, (c, m) in enumerate(GROUPS):
                    if m == 0:
                        dve.wait_ge(turn_taken, n * STAGE_TURNS + TURNS * (c + 1))
                    g = len(lefts(c, m))
                    dve.wait_ge(t_ready, n * NG + k + 1)
                    if PROD_LAST[k] >= 0 or not first:
                        dve.wait_ge(prod_used, n * NG + PROD_LAST[k] + 1)
                    nc.vector.tensor_tensor(
                        prod[:, PROD_SLOT[k], 0:g, :], t_ps[T_SLOT[k]][:, 0:g, :],
                        right[:, right_slot(c), :].unsqueeze(1).to_broadcast([P, g, TB]),
                        ALU.mult).then_inc(prod_ready, 1)
                    if first and k in PARTS_BEFORE:
                        weights_lo(PARTS_BEFORE[k])
                    if k in PARTS_AT and not (last and PARTS_AT[k] >= STAGES):
                        rows_lo(n, PARTS_AT[k])
                    if first and k in PARTS_AFTER:
                        weights_lo(PARTS_AFTER[k])

            for kind, x, _ in PROLOGUE:
                if kind == "weights":
                    weights_lo(x)
                elif kind == "rows":
                    rows_lo(0, x)
                elif kind == "piece" and not ON_ACT[x]:
                    take_piece(x)
            tile(0, True, False)
            with dve.Fori(1, TILES - 1) as n:
                tile(n, False, False)
            tile(TILES - 1, False, True)

        @block.tensor
        def _(pe):
            def fill_piece(p):
                c, i, first, chunks = PIECES[p]
                q = i + 1 - PER * c
                cols = slice(first * P, (first + chunks) * P)
                if p == 0 or PIECES[p - 1][0] != c:
                    pe.wait_ge(w_lo_made, made(c))
                before_it = [x for x in range(p) if PIECE_BANK[x] == PIECE_BANK[p]]
                if before_it:
                    wait_pieces(pe, before_it[-1] + 1)
                to = piece_bank(p)
                for of, window in ((hi, PER * q + 2), (lo, PER * q)):
                    last = nc.tensor.matmul(to, copy2[:, window * DIM:(window + PER) * DIM], of[c][:, cols],
                                            start=(of is hi), stop=(of is lo))
                last.then_inc(piece_filled, 1)

            def transform(n, first, k):
                c, m = GROUPS[k]
                if m == 0:
                    pe.wait_ge(turn_taken, n * STAGE_TURNS + TURNS * c + TURNS - 1)
                    if first:
                        if c < PE_BATCHES:
                            wait_pieces(pe, PIECES_TO[max(c, 2)])
                        else:
                            pe.wait_ge(lo_placed[c % 2], placed(c))
                            pe.wait_ge(hi_placed[c % 2], placed(c))
                if T_LAST[k] >= 0 or not first:
                    pe.wait_ge(prod_ready, n * NG + T_LAST[k] + 1)
                for i in lefts(c, m):
                    last = nc.tensor.matmul(t_ps[T_SLOT[k]][:, i % PER, :], w_split[:, chunk_at(i, c), :],
                                            stack[:, i, :], start=True, stop=True)
                last.then_inc(t_ready, 1)

            def sum_products(n, first, k):
                c, m = GROUPS[k]
                t, z_slot = divmod(k, Z_SLOTS)
                pe.wait_ge(prod_ready, n * NG + k + 1)
                if z_slot == 0 and not (first and t == 0):
                    pe.wait_ge(z_taken, n * Z_BLOCKS + t)
                in_block = range(Z_SLOTS * t, min(Z_SLOTS * t + Z_SLOTS, NG))
                for i in lefts(c, m):
                    a = i % PER
                    at = [x for x in in_block if len(lefts(*GROUPS[x])) > a]
                    last = nc.tensor.matmul(
                        z_ps[a * DIM:(a + 1) * DIM, 0, :], ones[:, z_slot, :], prod[:, PROD_SLOT[k], a, :],
                        start=(k == at[0]), stop=(k == at[-1] and (t < Z_BLOCKS - 1 or k == NG - 1)),
                        tile_position=(0, a * DIM))
                last.then_inc(prod_used, 1)

            def add_dense(n):
                pe.wait_ge(dense_loaded, n * 16 * HALVES + 16 * HALVES)
                for h in range(HALVES):
                    for a in range(PER):
                        last = nc.tensor.matmul(
                            z_ps[a * DIM:(a + 1) * DIM, 0, h * P:(h + 1) * P],
                            dense_pad[:, h, a, :], ident, start=False,
                            stop=(h == HALVES - 1 and a not in [i % PER for i in lefts(*GROUPS[-1])]),
                            tile_position=(0, a * DIM))
                last.then_inc(dense_used, 1)

            def turn(n, c, x):
                pe.wait_ge(hilo_ready, n * STAGES + c + 1)
                src_c, i = c % STAGES, PER * (c % STAGES) + 2 * x
                if x < TURNS - 1:
                    for d in range(min(2, LEFTS - i)):
                        for h in range(HALVES):
                            src = hilo[:, c % 2, h * PER + 2 * x + d].rearrange("p r q e -> p (r q e)")
                            last = nc.tensor.transpose(
                                aux_ps[:, d, h * P:(h + 1) * P].bitcast(FP32R), src, ident_r[:, :])
                else:
                    for h in range(HALVES):
                        last = nc.tensor.transpose(aux_ps[:, 0, h * P:(h + 1) * P],
                                                   rows[:, src_c, h, :], ident)
                last.then_inc(turned, 1)

            def hid1(t, m):
                return nc.tensor.matmul(h1_ps[:, m, :], w1[:, t, m * P:(m + 1) * P], z[:, t % Z_RING, :],
                                        start=(t == 0 and m % 2 == 0), stop=(t == Z_BLOCKS - 1),
                                        skip_group_check=True)

            def hid2(m, t, to=aux_ps[:, 0, :]):
                return nc.tensor.matmul(to, w2[t // 2][:, t % 2, m * P:(m + 1) * P], h1[:, t, :],
                                        start=(t == 0), stop=(t == HID1 // P - 1))

            def out_row(t):
                return nc.tensor.matmul(aux_ps[0:1, 0, :], w3[:, t:t + 1], h2[:, t, :],
                                        start=(t == 0), stop=(t == HID2 // P - 1))

            def first_layer(n, first, t, m, before):
                if m == 0:
                    if first and t == 0:
                        pe.wait_ge(w1_loaded, 16 * Z_BLOCKS)
                    pe.wait_ge(z_taken, (n - before) * Z_BLOCKS + t + 1)
                    if t == 0 and not first:
                        pe.wait_ge(h1_taken, n)
                last = hid1(t, m)
                if m == HID1 // P - 1:
                    last.then_inc(z_used, 1)

            def tail(n, kind, m, t):
                if t == 0:
                    if kind == "out":
                        pe.wait_ge(tail_taken, n * TAIL - 1)
                    elif m == 0:
                        pe.wait_ge(h1_taken, n)
                    else:
                        pe.wait_ge(tail_taken, n * TAIL + m - TAIL)
                last = hid2(m, t) if kind == "hid2" else out_row(t)
                if t == (HID1 if kind == "hid2" else HID2) // P - 1:
                    last.then_inc(tail_filled, 1)

            def tile(n, first, last_tile):
                tail_before = False
                taken = 0
                for k, (c, m) in enumerate(GROUPS):
                    transform(n, first, k)
                    if k >= 2:
                        sum_products(n, first, k - 2)
                    elif k == 0 and not first:
                        sum_products(n - 1, False, NG - 1)
                    for kind, x, y_ in JOBS[first, last_tile][k]:
                        if kind == "piece":
                            fill_piece(x)
                        elif kind == "turn":
                            pe.wait_ge(turn_taken, n * STAGE_TURNS + TURNS * x + y_)
                            if tail_before:
                                pe.wait_ge(tail_taken, n * TAIL + taken - TAIL)
                                tail_before = False
                            turn(n, x, y_)
                        elif kind in ("hid1", "hid1_before"):
                            first_layer(n, first, x, y_, before=(kind == "hid1_before"))
                        else:
                            if not tail_before:
                                turns = sum(j[0] == "turn" for kk in range(k + 1)
                                            for j in JOBS[first, last_tile][kk])
                                pe.wait_ge(turn_taken, n * STAGE_TURNS + TURNS_BEFORE + turns)
                            tail(n, kind, x, y_)
                            tail_before = True
                            taken = x + 1 if kind == "hid2" else TAIL
                sum_products(n, first, NG - 2)
                add_dense(n)

            pe.wait_ge(consts_loaded, 16)
            pe.wait_ge(copy2_ready, 1)
            for kind, x, y_ in PROLOGUE:
                if kind == "piece":
                    fill_piece(x)
                elif kind == "turn":
                    if x or y_:
                        pe.wait_ge(turn_taken, TURNS * x + y_)
                    turn(0, x, y_)
            tile(0, True, False)
            pe.wait_ge(mlp_loaded, 16 * MLP_LOADS)
            with pe.Fori(1, TILES - 1) as n:
                tile(n, False, False)
            tile(TILES - 1, False, True)
            sum_products(TILES - 1, False, NG - 1)
            pe.wait_ge(z_taken, TILES * Z_BLOCKS)
            for m in range(HID1 // P):
                last = hid1(Z_BLOCKS - 1, m)
                if m % 2 == 1:
                    last.then_inc(last_h1_summed, 1)
            pe.wait_ge(turn_taken, TILES * STAGE_TURNS)
            for t in range(HID1 // P):
                if t % 2 == 0:
                    pe.wait_ge(last_h1_taken, t // 2 + 1)
                for m in range(HID2 // P):
                    last = hid2(m, t, last_hid2_ps[m])
                    if t == HID1 // P - 1:
                        last.then_inc(tail_filled, 1)
            for t in range(HID2 // P):
                tail(TILES, "out", 0, t)


def kernel(**inputs):
    import concourse.bacc as bacc
    from concourse.bass_utils import run_bass_kernel_spmd

    nc = bacc.Bacc("TRN2", target_bir_lowering=False, num_devices=1, dynamic_dma_scratch_size=SCRATCH)
    names = ["ids"] + [f"tbl_{f}" for f in range(FIELDS)] + [
        "dense_ctx", "L0_rec_W", "W_top1", "b_top1", "W_top2", "b_top2", "W_top3"]
    arrays = {f"in_{name}": np.ascontiguousarray(inputs[name]) for name in names}
    arrays |= {f"const_{name}": a for name, a in constants().items()}
    args = [nc.dram_tensor(name, a.shape, mybir.dt.from_np(a.dtype), kind="ExternalInput").ap()
            for name, a in arrays.items()]
    out = nc.dram_tensor("out", (BATCH, 1), FP32, kind="ExternalOutput").ap()
    dlrm_tower_kernel(nc, args[0], args[1:1 + FIELDS], *args[1 + FIELDS:], out)
    r = run_bass_kernel_spmd(nc, [arrays], core_ids=[0])
    return r.results[0]["out"]
```
